# Optimizing a Trainium2 kernel written in Bass

```python
import numpy as np
import jax
import jax.numpy as jnp

def _softmax(x, axis=-1):
    return jax.nn.softmax(x, axis=axis)

def _gelu(x):
    return jax.nn.gelu(x, approximate=True)

def _silu(x):
    return jax.nn.silu(x)

def _sigmoid(x):
    return jax.nn.sigmoid(x)

def _layernorm(x, axis=-1, eps=1e-05):
    m = jnp.mean(x, axis=axis, keepdims=True)
    v = jnp.var(x, axis=axis, keepdims=True)
    return (x - m) / jnp.sqrt(v + eps)

def _scatter_add(tgt, idx, src, axis=0):
    return tgt.at[idx].add(src)

def _segment_sum(src, seg, n):
    return jax.ops.segment_sum(src, seg, n)
kernel_name = 'mk_conv_preact_d2_conv_nchw192_r2_2d288c'

def setup_inputs(seed: int=0):
    np.random.seed(seed)
    _w = jnp.asarray

    def _rec_inputs():
        import jax
        import jax.numpy as jnp
        _gk = jax.random.key(seed)
        x = -1.8e-05 + 0.9999 * jax.random.normal(jax.random.fold_in(_gk, 1), (8, 96, 96, 96), jnp.float32)
        return x
    x = _rec_inputs()

    def _L0_conv_setup():
        import jax, jax.numpy as jnp
        import numpy as np
        from jax import lax
        DIM = 96
        MID = max(DIM // 2, 4)
        B, H, W = (8, 96, 96)
        DN = ('NCHW', 'OIHW', 'NCHW')

        def _dwconv(x, w, pad):
            return lax.conv_general_dilated(x, w, (1, 1), pad, dimension_numbers=DN, feature_group_count=DIM)
        key = jax.random.key(seed)
        ks = jax.random.split(key, 8)
        s = 0.05
        return {'x': jax.random.normal(ks[0], (B, DIM, H, W), jnp.float32), 'w_h': jax.random.normal(ks[1], (DIM, 1, 1, 7), jnp.float32) * s, 'w_v': jax.random.normal(ks[2], (DIM, 1, 7, 1), jnp.float32) * s, 'w_d45': jax.random.normal(ks[3], (DIM, 1, 7, 7), jnp.float32) * s, 'w_d135': jax.random.normal(ks[4], (DIM, 1, 7, 7), jnp.float32) * s, 'w_att1': jax.random.normal(ks[5], (MID, 4 * DIM), jnp.float32) * s, 'w_att2': jax.random.normal(ks[6], (4 * DIM, MID), jnp.float32) * s, 'w_proj': jax.random.normal(ks[7], (DIM, DIM, 3, 3), jnp.float32) * s}
    _L0_conv_all = _L0_conv_setup()
    _L0_conv_in = {k: v for k, v in _L0_conv_all.items() if k in ('w_h', 'w_v', 'w_d45', 'w_d135', 'w_att1', 'w_att2', 'w_proj')}
    del _L0_conv_all

    def _L1_conv_setup():
        import jax, jax.numpy as jnp
        import numpy as np
        from jax import lax
        B, C, NH, HW = (4, 96, 4, 128)

        def conv1x1(x, w):
            return jnp.einsum('oc,bchw->bohw', w, x)

        def dwconv3x3(x, w):
            return lax.conv_general_dilated(x, w, window_strides=(1, 1), padding='SAME', feature_group_count=w.shape[0], dimension_numbers=('NCHW', 'OIHW', 'NCHW'))

        def _l2norm(t, eps=1e-12):
            return t / jnp.maximum(jnp.linalg.norm(t, axis=-1, keepdims=True), eps)
        key = jax.random.key(seed)
        ks = jax.random.split(key, 9)
        s = 0.02
        return {'x': jax.random.normal(ks[0], (B, C, HW, HW), jnp.float32), 'temperature': jnp.ones((1, NH, 1, 1), jnp.float32), 'w_qkv': jax.random.normal(ks[1], (3 * C, C), jnp.float32) * s, 'w_proj': jax.random.normal(ks[2], (C, C), jnp.float32) * s, 'w_kv': jax.random.normal(ks[3], (2 * C, C), jnp.float32) * s, 'w_q1': jax.random.normal(ks[4], (C, C), jnp.float32) * s, 'w_q2': jax.random.normal(ks[5], (C, C), jnp.float32) * s, 'w_kvconv': jax.random.normal(ks[6], (2 * C, 1, 3, 3), jnp.float32) * s, 'w_projf': jax.random.normal(ks[7], (C, C), jnp.float32) * s}
    _L1_conv_all = _L1_conv_setup()
    _L1_conv_in = {k: v for k, v in _L1_conv_all.items() if k in ('temperature', 'w_qkv', 'w_proj', 'w_kv', 'w_q1', 'w_q2', 'w_kvconv', 'w_projf')}
    del _L1_conv_all
    return {'x': x, 'L0_conv_w_h': _L0_conv_in['w_h'], 'L0_conv_w_v': _L0_conv_in['w_v'], 'L0_conv_w_d45': _L0_conv_in['w_d45'], 'L0_conv_w_d135': _L0_conv_in['w_d135'], 'L0_conv_w_att1': _L0_conv_in['w_att1'], 'L0_conv_w_att2': _L0_conv_in['w_att2'], 'L0_conv_w_proj': _L0_conv_in['w_proj'], 'L1_conv_temperature': _L1_conv_in['temperature'], 'L1_conv_w_qkv': _L1_conv_in['w_qkv'], 'L1_conv_w_proj': _L1_conv_in['w_proj'], 'L1_conv_w_kv': _L1_conv_in['w_kv'], 'L1_conv_w_q1': _L1_conv_in['w_q1'], 'L1_conv_w_q2': _L1_conv_in['w_q2'], 'L1_conv_w_kvconv': _L1_conv_in['w_kvconv'], 'L1_conv_w_projf': _L1_conv_in['w_projf']}

def reference(x, L0_conv_w_h, L0_conv_w_v, L0_conv_w_d45, L0_conv_w_d135, L0_conv_w_att1, L0_conv_w_att2, L0_conv_w_proj, L1_conv_temperature, L1_conv_w_qkv, L1_conv_w_proj, L1_conv_w_kv, L1_conv_w_q1, L1_conv_w_q2, L1_conv_w_kvconv, L1_conv_w_projf):
    import jax
    import jax.numpy as jnp

    def _L0_conv_ref(x, w_h, w_v, w_d45, w_d135, w_att1, w_att2, w_proj):
        import jax, jax.numpy as jnp
        import numpy as np
        from jax import lax
        DIM = 96
        MID = max(DIM // 2, 4)
        B, H, W = (8, 96, 96)
        DN = ('NCHW', 'OIHW', 'NCHW')

        def _dwconv(x, w, pad):
            return lax.conv_general_dilated(x, w, (1, 1), pad, dimension_numbers=DN, feature_group_count=DIM)
        diag = jnp.eye(7, dtype=x.dtype)
        anti = jnp.fliplr(diag)
        feat_h = _dwconv(x, w_h, ((0, 0), (3, 3)))
        feat_v = _dwconv(x, w_v, ((3, 3), (0, 0)))
        feat_d45 = _dwconv(x, w_d45 * diag, ((3, 3), (3, 3)))
        feat_d135 = _dwconv(x, w_d135 * anti, ((3, 3), (3, 3)))
        feats = jnp.stack([feat_h, feat_v, feat_d45, feat_d135], axis=1)
        context = jnp.mean(feats * feats, axis=(3, 4)).reshape(x.shape[0], -1)
        hid = jax.nn.leaky_relu(context @ w_att1.T, negative_slope=0.2)
        attn = (hid @ w_att2.T).reshape(x.shape[0], 4, DIM)
        attn = jax.nn.softmax(attn, axis=1)[..., None, None]
        feat_geom = jnp.sum(attn * feats, axis=1)
        return lax.conv_general_dilated(feat_geom, w_proj, (1, 1), ((1, 1), (1, 1)), dimension_numbers=DN)

    def _L1_conv_ref(x, temperature, w_qkv, w_proj, w_kv, w_q1, w_q2, w_kvconv, w_projf):
        import jax, jax.numpy as jnp
        import numpy as np
        from jax import lax
        B, C, NH, HW = (4, 96, 4, 128)

        def conv1x1(x, w):
            return jnp.einsum('oc,bchw->bohw', w, x)

        def dwconv3x3(x, w):
            return lax.conv_general_dilated(x, w, window_strides=(1, 1), padding='SAME', feature_group_count=w.shape[0], dimension_numbers=('NCHW', 'OIHW', 'NCHW'))

        def _l2norm(t, eps=1e-12):
            return t / jnp.maximum(jnp.linalg.norm(t, axis=-1, keepdims=True), eps)
        b, c, h, w = x.shape
        nh = temperature.shape[1]
        d = c // nh
        N = h * w
        q, k, v = jnp.split(conv1x1(x, w_qkv), 3, axis=1)
        q = jax.nn.softmax(q.reshape(b, nh, d, N), axis=-1)
        k = jax.nn.softmax(k.reshape(b, nh, d, N), axis=-1)
        v = v.reshape(b, nh, d, N)
        context = jnp.einsum('bhdn,bhen->bhde', k, v)
        out = jnp.einsum('bhde,bhdn->bhen', context, q).reshape(b, c, h, w)
        out = conv1x1(out, w_proj)
        x_fft = jnp.fft.fftn(x, axes=(-2, -1)).real
        x_mid = jax.nn.gelu(conv1x1(x_fft, w_q1), approximate=False)
        qf = jnp.fft.ifftn(conv1x1(x_mid, w_q2), axes=(-2, -1)).real
        kf, vf = jnp.split(dwconv3x3(conv1x1(out, w_kv), w_kvconv), 2, axis=1)
        qf = _l2norm(qf.reshape(b, nh, d, N))
        kf = _l2norm(kf.reshape(b, nh, d, N))
        vf = vf.reshape(b, nh, d, N)
        attnf = jax.nn.softmax(jnp.einsum('bhdn,bhen->bhde', qf, k) * temperature, axis=-1)
        outf = jnp.einsum('bhde,bhen->bhdn', attnf, vf).reshape(b, c, h, w)
        return conv1x1(outf, w_projf)

    def _gn(v, G=32, eps=1e-05):
        B_, C_, H_, W_ = v.shape
        g = v.reshape(B_, G, C_ // G, H_, W_)
        m = jnp.mean(g, axis=(2, 3, 4), keepdims=True)
        s = jnp.var(g, axis=(2, 3, 4), keepdims=True)
        return ((g - m) / jnp.sqrt(s + eps)).reshape(v.shape)

    def _ln_c(v, eps=1e-06):
        m = jnp.mean(v, axis=1, keepdims=True)
        s = jnp.var(v, axis=1, keepdims=True)
        return (v - m) / jnp.sqrt(s + eps)

    def _ln_t(v, eps=1e-05):
        m = jnp.mean(v, axis=-1, keepdims=True)
        s = jnp.var(v, axis=-1, keepdims=True)
        return (v - m) / jnp.sqrt(s + eps)

    def _to_tokens(v):
        B_, C_, H_, W_ = v.shape
        return v.reshape(B_, C_, H_ * W_).transpose(0, 2, 1)

    def _from_tokens(t, like):
        B_, C_, H_, W_ = like.shape
        return t.transpose(0, 2, 1).reshape(B_, C_, H_, W_)
    x = x + _L0_conv_ref(_gn(x), L0_conv_w_h, L0_conv_w_v, L0_conv_w_d45, L0_conv_w_d135, L0_conv_w_att1, L0_conv_w_att2, L0_conv_w_proj)
    x = x + _L1_conv_ref(_gn(x), L1_conv_temperature, L1_conv_w_qkv, L1_conv_w_proj, L1_conv_w_kv, L1_conv_w_q1, L1_conv_w_q2, L1_conv_w_kvconv, L1_conv_w_projf)
    return x

_drawn_inputs = setup_inputs


def setup_inputs(seed=0):
    import zlib

    import numpy as np

    out = dict(_drawn_inputs(seed))
    spreads = {'L1_conv_temperature': (1.0, 0.2)}
    factors = {'L0_conv_w_att1': 22.074, 'L0_conv_w_att2': 8.0}
    for name, (base, spread) in spreads.items():
        noise = np.random.default_rng([zlib.crc32(name.encode()), seed]).standard_normal(out[name].shape)
        drawn = base * np.exp(spread * noise) if base else spread * noise
        out[name] = jnp.asarray(drawn.astype(out[name].dtype))
    for name, factor in factors.items():
        out[name] = (out[name] * factor).astype(out[name].dtype)
    return out
```

```python
from contextlib import ExitStack

import concourse.bass as bass
from concourse import mybir

F32 = mybir.dt.float32
F32R = mybir.dt.float32r
ALU = mybir.AluOpType
ACT = mybir.ActivationFunctionType
AX = mybir.AxisListType

B, C, H, W = 8, 96, 96, 96
N = H * W
HEADS, HD = 4, 24
MID = 48
DIRS, KT = 4, 7
PAD = KT // 2
CR = 16
NCH = H // CR
XR, XP = CR + 2 * PAD, W + 2 * PAD
GR = 8
NG = H // GR
TR = 4
EP = W + 1
EN = (H + 2) * EP + 2
NV = W // 2 + 1
BANK = 512
SLOTS = 3
RES = 3
STATS = N // BANK
XSTAT = CR * W // BANK

U_MAX = 2 * STATS
U_ROWS = H // TR
U_DFT = C // 4 + C // 8
U_KV = H // 2
U_E = H // TR
AT_ROWS = U_MAX
AT_DFT1 = AT_ROWS + U_ROWS
AT_KV = AT_DFT1 + U_DFT
AT_DFT2 = AT_KV + U_KV
AT_E = AT_DFT2 + U_DFT
USES = AT_E + U_E
assert USES % SLOTS == 0

DFT_ORDER = []
for _j in range(C // 8 + 1):
    if _j < C // 8:
        DFT_ORDER += [(1, 2 * _j), (1, 2 * _j + 1)]
    if _j >= 1:
        DFT_ORDER.append((2, _j - 1))
assert len(DFT_ORDER) == U_DFT

PADS = 6
TAPS = DIRS * KT
L0_SMALL, L1_SMALL, GN_SMALL = 8, 21, 7


def tap_shift(d, k):
    s = k - PAD
    return [(0, s), (s, 0), (s, s), (s, -s)][d]


def build(nc, a, out):
    with ExitStack() as ctx:
        def sb(name, shape, dt=F32):
            return ctx.enter_context(nc.sbuf_tensor(name, shape, dt))

        def sem(name):
            return ctx.enter_context(nc.semaphore(name))

        EBYTES = -(-EN * 4 // 32) * 32
        arena = sb("arena", [128, 2 * EBYTES // 4])
        lo0 = nc.sbuf_base - 2 * EBYTES
        e_hi = nc.alloc_sbuf_tensor_at("e_hi", [C, EN], F32R, offset=lo0)
        e_lo = nc.alloc_sbuf_tensor_at("e_lo", [C, EN], F32R, offset=lo0 + EBYTES)
        z = nc.alloc_sbuf_tensor_at("z", [W, H, C], F32, offset=lo0)
        t_sp = nc.alloc_sbuf_tensor_at("t_sp", [H, NV, 2 * C], F32, offset=lo0 + H * C * 4)
        assert (H * C + NV * 2 * C) * 4 <= 2 * EBYTES
        SBYTES = CR * W * 4
        arena2 = sb("arena2", [128, SBYTES // 4])
        s0 = nc.sbuf_base - SBYTES
        s1 = nc.alloc_sbuf_tensor_at("s1", [H, 2, 8, W], F32, offset=s0)
        a32 = nc.alloc_sbuf_tensor_at("a32", [C, 9, C], F32, offset=s0)
        acc = nc.alloc_sbuf_tensor_at("acc", [C, CR, W], F32, offset=s0)

        x1 = sb("x1", [C + 1, N])
        xin = sb("xin", [C, 2, XR, XP])
        feat = sb("feat", [C, DIRS, CR * W])
        res = sb("res", [C, RES, GR * W])
        vrow = sb("vrow", [W, 4, 2, C])
        etile = sb("etile", [C, 2, TR * W])
        wp_hi, wp_lo = sb("wp_hi", [C, 9, C], F32R), sb("wp_lo", [C, 9, C], F32R)
        a_hi, a_lo = sb("a_hi", [C, 9, C], F32R), sb("a_lo", [C, 9, C], F32R)
        bk = sb("bk", [C, 9, C])
        wkv = sb("wkv", [C + 1, 2 * C])
        mats = sb("mats", [C, 12, C])
        ident, group, mask, negmask, w_dft, dcos, dnsin, wq, wq1, wq2, wq2t, wpft = (
            mats[:, i, :] for i in range(12))
        wc = sb("wc", [C, C])
        wh, wv = sb("wh", [C, KT]), sb("wv", [C, KT])
        w45, w135 = sb("w45", [C, KT * KT]), sb("w135", [C, KT * KT])
        wk3, temp = sb("wk3", [C, 9]), sb("temp", [C, 1])
        att1, att2 = sb("att1", [C, DIRS, MID]), sb("att2", [MID, DIRS * C])
        stat, mv, gstat, gpar = sb("stat", [C, 24, 6]), sb("mv", [C, 2]), sb("gstat", [C, 2]), sb("gpar", [C, 4])
        xpar, x1par = sb("xpar", [C, 2]), sb("x1par", [C, 2])
        consts = sb("consts", [C, 2])
        one = sb("one", [C, 1])
        sq = sb("sq", [C, DIRS, NCH])
        sqjunk = sb("sqjunk", [C, CR * W], mybir.dt.bfloat16)
        l0v = sb("l0v", [C, 20])
        hid = sb("hid", [MID, 2])
        mx = sb("mx", [C, 2, STATS])
        nmax = sb("nmax", [C, 2])
        zq = sb("zq", [C, U_E])
        l1v = sb("l1v", [C, 16])
        gram, gram0 = sb("gram", [C, 2 * C]), sb("gram0", [C, 2 * C])
        ctxm, s_t, m_b, att_f, junk = (sb(n, [C, C]) for n in ("ctxm", "s_t", "m_b", "att_f", "junk"))

        conv_ps = ctx.enter_context(nc.psum_tensor("conv_ps", [128, 2, 2, BANK], F32))
        stage_ps = ctx.enter_context(nc.psum_tensor("stage_ps", [128, SLOTS, BANK], F32))
        small_ps = ctx.enter_context(nc.psum_tensor("small_ps", [128, BANK], F32))
        ctx_ps, gram_ps, a_ps = conv_ps[:, 0, 0], conv_ps[:, 0, 1], conv_ps[:, 1]

        feats_d = nc.dram_tensor("feats_d", (DIRS, C, N), F32, kind="Internal").ap()
        x1_d = nc.dram_tensor("x1_d", (C, N), F32, kind="Internal").ap()

        w_loaded = sem("w_loaded")
        xin_loaded = [sem(f"xin_loaded{i}") for i in range(2)]
        feat_loaded = [sem(f"feat_loaded{i}") for i in range(DIRS)]
        feat_stored = [sem(f"feat_stored{i}") for i in range(DIRS)]
        res_loaded = [sem(f"res_loaded{i}") for i in range(RES)]
        out_stored = [sem(f"out_stored{i}") for i in range(RES)]
        x1_stored = sem("x1_stored")
        zeroed, consts_set, wc_ready, wc_copied, wp_hi_ready, wp_ready = map(sem, (
            "zeroed", "consts_set", "wc_ready", "wc_copied", "wp_hi_ready", "wp_ready"))
        x_stat = sem("x_stat")
        gnx_small, gnx1_small = sem("gnx_small"), sem("gnx1_small")
        gnx_ps, gnx1_ps = sem("gnx_ps"), sem("gnx1_ps")
        gnx_pow, gnx1_pow = sem("gnx_pow"), sem("gnx1_pow")
        xin_ready = sem("xin_ready")
        edge_zero = sem("edge_zero")
        tap_done = sem("tap_done")
        squared = sem("squared")
        l0_small, l0_ps, l0_exp = sem("l0_small"), sem("l0_ps"), sem("l0_exp")
        combo = sem("combo")
        fg_hi, fg_ready = sem("fg_hi"), sem("fg_ready")
        conv_ready = sem("conv_ready")
        x1_done, x1_stat = sem("x1_done"), sem("x1_stat")
        xn_ready = sem("xn_ready")
        stage_full = sem("stage_full")
        max_part = sem("max_part")
        stage_evac = sem("stage_evac")
        l1_small, l1_ps = sem("l1_small"), sem("l1_ps")
        maxrow_ready, gram_done, l1_pow, l1_exp = map(sem, ("maxrow_ready", "gram_done", "l1_pow", "l1_exp"))
        pads_zero, e_hi_ready, e_ready, a_hi_ready = map(sem, ("pads_zero", "e_hi_ready", "e_ready", "a_hi_ready"))
        fin_ready, out_done = sem("fin_ready"), sem("out_done")
        waits_passed = {e.engine: sem(n) for e, n in (
            (nc.sync, "sp_passed"), (nc.gpsimd, "pool_passed"), (nc.vector, "dve_passed"))}

        block = ctx.enter_context(nc.Block())

        def wait(eng, s, value):
            if not isinstance(value, int) or value > 0:
                eng.wait_ge(s, value)

        def apart(eng):
            eng.sem_inc(waits_passed[eng.engine], 1)

        def rows(buf, r0, n, dx=0):
            at = (r0 + 1) * EP + 1 + dx
            return buf[:, at:at + n * EP].rearrange("p (r c) -> p r c", c=EP)[:, :, 0:W]

        def small_chain(eng, s, total, i):
            state = [0]

            def step(ins):
                state[0] += 1
                assert state[0] <= total
                ins.then_inc(s, 1)
                eng.wait_ge(s, i * total + state[0])
            return step

        nstat = [len([n for n in range(NCH) if n % DIRS == s]) for s in range(DIRS)]
        per_slot = [nstat[s] + NCH for s in range(DIRS)]

        def stat_loaded(b, n):
            s = n % DIRS
            return feat_loaded[s], (b * per_slot[s] + n // DIRS + 1) * 16

        def combo_loaded(b, ch, d):
            return feat_loaded[d], (b * per_slot[d] + nstat[d] + ch + 1) * 16

        def res_use(i, j, final):
            n = (NG if final else 0) + j
            return n % RES, (i * (2 * NG // RES) + n // RES + 1) * 16

        def wait_res_free(eng, i, j, final):
            n = (NG if final else 0) + j - RES
            if n < 0:
                wait(eng, out_stored[j % RES], i * (NG // RES) * 16)
            elif n < NG:
                wait(eng, x1_done, i * NG + n + 1)
            else:
                wait(eng, out_stored[n % RES], (i * (NG // RES) + (n - NG) // RES + 1) * 16)

        def image(t, i):
            return t[i] if isinstance(i, int) else t[bass.ds(i, 1)].rearrange("a c n -> (a c) n")

        def steps(eng, step):
            step(0, True, False)
            with eng.Fori(1, B) as b:
                step(b, True, True)
            step(B, False, True)

        @block.sync
        def _(sp):
            loads = [(mats[:, n, :], a[k]) for n, k in enumerate(
                ("ident", "group", "mask", "negmask", "w_dft", "dcos", "dnsin", "wq", "wq1", "wq2", "wq2t", "wpft"))]
            loads += [(wkv[0:C, :], a["wkv"]), (wh[:], a["wh"]), (wv[:], a["wv"]), (w45[:], a["w45"]),
                      (w135[:], a["w135"]), (wk3[:], a["wk3"]), (temp[:], a["temp"]), (att1[:], a["att1"]),
                      (att2[:], a["att2"]), (a32[:], a["wp"]), (m_b[:], a["w_mid"]), (s_t[:], a["wkvv"])]
            for dst, src in loads:
                sp.dma_start(dst, src).then_inc(w_loaded, 16)

            def step(b, first, second):
                if not first:
                    return
                x = image(a["x"], b)
                for n in range(NCH):
                    s = n % DIRS
                    if n < DIRS:
                        wait(sp, combo, b * DIRS * NCH)
                    else:
                        wait(sp, x_stat, b * STATS + (n - DIRS + 1) * XSTAT)
                    sp.dma_start(feat[:, s], x[:, n * CR * W:(n + 1) * CR * W]).then_inc(feat_loaded[s], 16)

                def load_xin(ch):
                    lo, hi = max(0, ch * CR - PAD), min(H, ch * CR + CR + PAD)
                    at = lo - (ch * CR - PAD)
                    if ch < 2:
                        wait(sp, tap_done, b * NCH * TAPS - (1 - ch) * TAPS)
                    else:
                        wait(sp, tap_done, b * NCH * TAPS + (ch - 1) * TAPS)
                    if isinstance(b, int):
                        wait(sp, zeroed, 1)
                    sp.dma_start(xin[:, ch % 2, at:at + hi - lo, PAD:PAD + W],
                                 x[:, lo * W:hi * W].rearrange("c (r w) -> c r w", w=W)).then_inc(xin_loaded[ch % 2], 16)

                load_xin(0)
                load_xin(1)
                for ch in range(NCH):
                    for d in range(DIRS):
                        wait(sp, tap_done, b * NCH * TAPS + ch * TAPS + (d // 2) * 2 * KT + 2 * KT - 1 + d % 2)
                        sp.dma_start(feats_d[d, :, ch * CR * W:(ch + 1) * CR * W], feat[:, d]).then_inc(feat_stored[d], 16)
                    if ch + 2 < NCH:
                        load_xin(ch + 2)
                for ch in range(NCH):
                    for d in range(DIRS):
                        if ch == 0:
                            wait(sp, feat_stored[d], (b * NCH + NCH) * 16)
                            apart(sp)
                            wait(sp, squared, b * DIRS * NCH + DIRS * (NCH - 1) + d + 1)
                        else:
                            wait(sp, combo, (b * NCH + ch - 1) * DIRS + d + 1)
                        sp.dma_start(feat[:, d], feats_d[d, :, ch * CR * W:(ch + 1) * CR * W]).then_inc(feat_loaded[d], 16)
            steps(sp, step)

        @block.gpsimd
        def _(pool):
            def gn_pow(chain, per, i, at, col, done):
                wait(pool, chain, i * per + at)
                pool.tensor_tensor(gpar[:, col:col + 1], gpar[:, col:col + 1], consts[:, 0:1], ALU.pow).then_inc(done, 1)

            def zero_pads():
                for e in (e_hi, e_lo):
                    f = e[:, :].bitcast(F32)
                    pool.memset(f[:, 0:EP], 0.0).then_inc(pads_zero, 1)
                    pool.memset(f[:, (H + 1) * EP:EN], 0.0).then_inc(pads_zero, 1)
                    pool.memset(f[:, EP:EP + H * EP].rearrange("p (r c) -> p r c", c=EP)[:, :, 0:1], 0.0)\
                        .then_inc(pads_zero, 1)

            def step(b, first, second):
                if first:
                    gn_pow(gnx_small, GN_SMALL, b, 5, 0, gnx_pow)
                if second:
                    i = b - 1
                    pool.wait_ge(gram_done, i + 1)
                    apart(pool)
                    zero_pads()
                    pool.wait_ge(l1_small, i * L1_SMALL + 5)
                    pool.tensor_tensor(l1v[:, 1:2], l1v[:, 0:1], consts[:, 1:2], ALU.pow).then_inc(l1_pow, 1)
                    o = image(out, i)
                    for j in range(NG + 1):
                        if j < NG:
                            s, _n = res_use(i, j, True)
                            wait_res_free(pool, i, j, True)
                            if j == 0:
                                pool.wait_ge(x1_stored, (i * NG + NG) * 16)
                            apart(pool)
                            pool.dma_start(res[:, s], x1_d[:, j * GR * W:(j + 1) * GR * W]).then_inc(res_loaded[s], 16)
                        if j >= 1:
                            s, _n = res_use(i, j - 1, True)
                            pool.wait_ge(out_done, i * NG + j)
                            apart(pool)
                            pool.dma_start(o[:, (j - 1) * GR * W:j * GR * W], res[:, s]).then_inc(out_stored[s], 16)
                if first:
                    if not second:
                        zero_pads()
                    x = image(a["x"], b)
                    for j in range(NG + 1):
                        if j < NG:
                            s, _n = res_use(b, j, False)
                            wait_res_free(pool, b, j, False)
                            apart(pool)
                            pool.dma_start(res[:, s], x[:, j * GR * W:(j + 1) * GR * W]).then_inc(res_loaded[s], 16)
                        if j >= 1:
                            pool.wait_ge(x1_done, b * NG + j)
                            apart(pool)
                            pool.dma_start(x1_d[:, (j - 1) * GR * W:j * GR * W], x1[0:C, (j - 1) * GR * W:j * GR * W])\
                                .then_inc(x1_stored, 16)
                    gn_pow(gnx1_small, GN_SMALL, b, 5, 2, gnx1_pow)

            pool.memset(xin[:], 0.0).then_inc(zeroed, 1)
            pool.memset(x1[C:C + 1, :], 1.0).then_inc(consts_set, 1)
            pool.memset(wkv[C:C + 1, C:2 * C], 0.0).then_inc(consts_set, 1)
            pool.memset(one[:], 1.0).then_inc(consts_set, 1)
            pool.memset(consts[:, 0:1], -0.5).then_inc(consts_set, 1)
            pool.memset(consts[:, 1:2], 0.5).then_inc(consts_set, 1)
            pool.wait_ge(consts_set, 5)
            steps(pool, step)
            for s in range(RES):
                pool.wait_ge(out_stored[s], B * (NG // RES) * 16)

        @block.scalar
        def _(act):
            wp32 = a32
            act.wait_ge(w_loaded, 24 * 16)
            act.activation(wp_hi[:], wp32[:], ACT.Identity).then_inc(wp_hi_ready, 1)
            act.wait_ge(wc_ready, 1)
            act.activation(wc[:], small_ps[0:C, 0:C], ACT.Identity).then_inc(wc_copied, 1)

            def norm_chunk(b, ch):
                lo, hi = max(0, ch * CR - PAD), min(H, ch * CR + CR + PAD)
                at = lo - (ch * CR - PAD)
                if ch == 0:
                    act.wait_ge(gnx_small, b * GN_SMALL + GN_SMALL)
                act.wait_ge(xin_loaded[ch % 2], (b * (NCH // 2) + ch // 2 + 1) * 16)
                v = xin[:, ch % 2, at:at + hi - lo, PAD:PAD + W]
                act.activation(v, v, ACT.Identity, scale=xpar[:, 0:1], bias=xpar[:, 1:2]).then_inc(xin_ready, 1)

            def squares(b, ch, pair):
                for d in (2 * pair, 2 * pair + 1):
                    act.wait_ge(tap_done, b * NCH * TAPS + ch * TAPS + pair * 2 * KT + 2 * KT - 1 + d % 2)
                    wait(act, squared, b * DIRS * NCH + ch * DIRS + d)
                    act.activation(sqjunk[:], feat[:, d], ACT.Square, accum_out=sq[:, d, ch:ch + 1]).then_inc(squared, 1)

            def stage(i, u):
                act.wait_ge(stage_full, i * USES + u + 1)
                return stage_ps[:, u % SLOTS]

            def max_row(i):
                act.wait_ge(l1_ps, i * 5 + 1)
                act.activation(wkv[C:C + 1, 0:C], small_ps[0:1, 0:C], ACT.Identity).then_inc(maxrow_ready, 1)

            def u_rows(i):
                for g in range(U_ROWS):
                    ps = stage(i, AT_ROWS + g)
                    act.activation(z[:, g * TR:(g + 1) * TR, :], ps[0:W, 0:TR * C].rearrange("p (r c) -> p r c", c=C),
                                   ACT.Identity).then_inc(stage_evac, 1)

            def dft(i, at, ch0, func, between=None):
                for n, (kind, g) in enumerate(DFT_ORDER):
                    ps = stage(i, at + n)
                    if kind == 1:
                        act.activation(s1[:, (g // 2) % 2, (g % 2) * 4:(g % 2) * 4 + 4, :],
                                       ps[0:H, 0:4 * W].rearrange("p (c v) -> p c v", v=W), ACT.Identity).then_inc(stage_evac, 1)
                    else:
                        act.activation(t_sp[:, :, ch0 + 8 * g:ch0 + 8 * g + 8].rearrange("p v c -> p c v"),
                                       ps[0:H, 0:8 * NV].rearrange("p (c v) -> p c v", v=NV), func).then_inc(stage_evac, 1)

            def kv_rows(i, g0, g1):
                for g in range(g0, g1):
                    ps = stage(i, AT_KV + g)[0:W, 0:4 * C].rearrange("p (r c) -> p r c", c=2 * C)
                    act.activation(z[:, 2 * g:2 * g + 2, :], ps[:, :, 0:C], ACT.Exp)
                    act.activation(vrow[:, g % 4], ps[:, :, C:2 * C], ACT.Identity).then_inc(stage_evac, 1)

            def e_tiles(i, t0, t1):
                for t in range(t0, t1):
                    ps = stage(i, AT_E + t)
                    if t == 0:
                        act.wait_ge(pads_zero, (i + 2) * PADS)
                    if t >= 2:
                        act.wait_ge(e_ready, i * U_E + t - 1)
                    act.activation(etile[:, t % 2], ps[0:C, 0:TR * W], ACT.Exp, bias=nmax[:, 1:2],
                                   accum_out=zq[:, t:t + 1]).then_inc(stage_evac, 1)
                    act.wait_ge(stage_evac, i * (USES - U_MAX) + AT_E - U_MAX + t + 1)
                    act.activation(rows(e_hi, t * TR, TR), etile[:, t % 2].rearrange("p (r c) -> p r c", c=W),
                                   ACT.Identity).then_inc(e_hi_ready, 1)

            def attn_exp(i):
                act.wait_ge(l1_small, i * L1_SMALL + 13)
                act.activation(junk[:], gram0[:, 0:C], ACT.Exp, bias=l1v[:, 5:6], accum_out=l1v[:, 6:7]).then_inc(l1_exp, 1)

            def a_split(i):
                act.wait_ge(l1_small, i * L1_SMALL + 20)
                act.activation(a_hi[:], a32[:], ACT.Identity).then_inc(a_hi_ready, 1)

            def att_softmax(b):
                act.wait_ge(l0_small, b * L0_SMALL + 6)
                act.activation(l0v[:, 12:16], l0v[:, 4:8], ACT.Exp, bias=l0v[:, 16:17], accum_out=l0v[:, 17:18]).then_inc(l0_exp, 1)

            def fg_split(b):
                for ch in range(NCH):
                    act.wait_ge(combo, (b * NCH + ch + 1) * DIRS)
                    act.activation(rows(e_hi, ch * CR, CR), acc[:], ACT.Identity).then_inc(fg_hi, 1)

            def xn(b):
                act.wait_ge(gnx1_small, b * GN_SMALL + GN_SMALL)
                act.wait_ge(x1_stored, (b * NG + NG) * 16)
                for p in range(4):
                    v = x1[0:C, p * (N // 4):(p + 1) * (N // 4)]
                    act.activation(v, v, ACT.Identity, scale=x1par[:, 0:1], bias=x1par[:, 1:2]).then_inc(xn_ready, 1)

            def step(b, first, second):
                i = b - 1

                def l0(f, *args):
                    if first:
                        f(b, *args)

                def l1(f, *args):
                    if second:
                        f(i, *args)
                l1(max_row)
                l0(norm_chunk, 0)
                l0(norm_chunk, 1)
                l1(u_rows)
                l1(dft, AT_DFT1, 0, ACT.Gelu)
                l0(squares, 0, 0)
                l1(kv_rows, 0, U_KV // 2)
                l0(squares, 0, 1)
                l0(norm_chunk, 2)
                l1(kv_rows, U_KV // 2, U_KV)
                l0(squares, 1, 0)
                l1(dft, AT_DFT2, C, ACT.Identity)
                l0(squares, 1, 1)
                l0(norm_chunk, 3)
                l1(e_tiles, 0, 12)
                l1(attn_exp)
                l1(e_tiles, 12, U_E)
                l1(a_split)
                for ch in range(2, NCH):
                    l0(squares, ch, 0)
                    l0(squares, ch, 1)
                    if ch + 2 < NCH:
                        l0(norm_chunk, ch + 2)
                l0(att_softmax)
                l0(fg_split)
                l0(xn)
            steps(act, step)

        @block.vector
        def _(dve):
            taps_w = [lambda k: wh[:, k:k + 1], lambda k: wv[:, k:k + 1],
                      lambda k: w45[:, k * KT + k:k * KT + k + 1],
                      lambda k: w135[:, k * KT + KT - 1 - k:k * KT + KT - k]]
            dve.wait_ge(w_loaded, 24 * 16)
            dve.wait_ge(wp_hi_ready, 1)
            dve.tensor_tensor(wp_lo[:], a32[:], wp_hi[:].bitcast(F32), ALU.subtract).then_inc(wp_ready, 1)
            dve.wait_ge(zeroed, 1)
            dve.wait_ge(consts_set, 5)

            def x_stats(b, n0, n1):
                for n in range(n0, n1):
                    ch, k = n // XSTAT, n % XSTAT
                    if k == 0:
                        s, v = stat_loaded(b, ch)
                        dve.wait_ge(s, v)
                    dve.bn_stats(stat[:, n, :], feat[:, ch % DIRS, k * BANK:(k + 1) * BANK]).then_inc(x_stat, 1)

            def group_norm(b, n_stats, chain, ps_sem, pow_sem, col, par, last_stat, last_count):
                st = small_chain(dve, chain, GN_SMALL, b)
                dve.wait_ge(last_stat, last_count)
                apart(dve)
                st(dve.bn_aggr(mv[:], stat[:, 0:n_stats, :]))
                st(dve.scalar_tensor_tensor(out=mv[:, 1:2], in0=mv[:, 0:1], scalar=mv[:, 0:1], in1=mv[:, 1:2],
                                            op0=ALU.mult, op1=ALU.add))
                dve.wait_ge(ps_sem, b + 1)
                st(dve.tensor_copy(gstat[:], small_ps[0:C, 500:502]))
                st(dve.tensor_scalar(gpar[:, 3:4], gstat[:, 0:1], gstat[:, 0:1], None, ALU.mult))
                st(dve.scalar_tensor_tensor(out=gpar[:, col:col + 1], in0=gstat[:, 1:2], scalar=1e-5, in1=gpar[:, 3:4],
                                            op0=ALU.add, op1=ALU.subtract))
                dve.wait_ge(pow_sem, b + 1)
                st(dve.tensor_copy(par[:, 0:1], gpar[:, col:col + 1]))
                st(dve.scalar_tensor_tensor(out=par[:, 1:2], in0=gstat[:, 0:1], scalar=-1.0, in1=par[:, 0:1],
                                            op0=ALU.mult, op1=ALU.mult))

            EDGES = 2
            edge = [0]

            def edge_rows(b, ch):
                at = 0 if ch == 0 else XR - PAD
                dve.memset(xin[:, ch % 2, at:at + PAD, :], 0.0).then_inc(edge_zero, 1)
                edge[0] += 1
                dve.wait_ge(edge_zero, b * EDGES + edge[0])

            def taps(b, ch, pair, hook=None):
                n = ch * TAPS + pair * 2 * KT
                if pair == 0:
                    if ch in (0, NCH - 1):
                        edge_rows(b, ch)
                    dve.wait_ge(xin_ready, b * NCH + ch + 1)
                for k in range(KT):
                    for d in (2 * pair, 2 * pair + 1):
                        dy, dx = tap_shift(d, k)
                        src = xin[:, ch % 2, PAD + dy:PAD + dy + CR, PAD + dx:PAD + dx + W]
                        dst = feat[:, d].rearrange("p (r c) -> p r c", c=W)
                        if k == 0:
                            if ch >= 1:
                                dve.wait_ge(squared, b * DIRS * NCH + DIRS * (ch - 1) + d + 1)
                                dve.wait_ge(feat_stored[d], (b * NCH + ch) * 16)
                            ins = dve.tensor_scalar(dst, src, taps_w[d](k), None, ALU.mult)
                        else:
                            dve.wait_ge(tap_done, b * NCH * TAPS + n + 2 * (k - 1) + d % 2 + 1)
                            ins = dve.scalar_tensor_tensor(out=dst, in0=src, scalar=taps_w[d](k), in1=dst,
                                                           op0=ALU.mult, op1=ALU.add)
                        ins.then_inc(tap_done, 1)
                    if hook and k == 3:
                        hook()
                if hook:
                    hook()

            def maxes(i, n0, n1):
                for n in range(n0, n1):
                    dve.wait_ge(stage_full, i * USES + n + 1)
                    dve.tensor_reduce(mx[:, n % 2, n // 2:n // 2 + 1], stage_ps[0:C, n % SLOTS, :], AX.X, ALU.max)\
                        .then_inc(max_part, 1)

            def e_split(i, t0, t1):
                for t in range(t0, t1):
                    dve.wait_ge(e_hi_ready, i * U_E + t + 1)
                    dve.tensor_tensor(rows(e_lo, t * TR, TR), etile[:, t % 2].rearrange("p (r c) -> p r c", c=W),
                                      rows(e_hi, t * TR, TR).bitcast(F32), ALU.subtract).then_inc(e_ready, 1)

            def attention_weights(i, chain):
                st = chain
                dve.wait_ge(gram_done, i + 1)
                st(dve.tensor_tensor(ctxm[:], ctx_ps[0:C, 0:C], mask, ALU.mult))
                st(dve.tensor_copy(gram0[:], gram_ps[0:C, 0:2 * C]))
                st(dve.scalar_tensor_tensor(out=gram[:], in0=gram_ps[0:C, 2 * C:4 * C], scalar=2.0, in1=gram0[:],
                                            op0=ALU.mult, op1=ALU.add))
                e_split(i, 0, 6)
                dve.wait_ge(l1_ps, i * 5 + 2)
                st(dve.tensor_tensor_reduce(junk[:], small_ps[0:C, 0:C], wq2, 1.0 / N, 0.0, ALU.mult, ALU.add,
                                            l1v[:, 0:1]))
                st(dve.reciprocal(l1v[:, 2:3], small_ps[0:C, 2 * C:2 * C + 1]))
                st(dve.tensor_scalar(s_t[:], small_ps[0:C, C:2 * C], l1v[:, 2:3], None, ALU.mult))
                st(dve.tensor_copy(m_b[:], ctx_ps[0:C, 128:128 + C]))
                dve.wait_ge(l1_pow, i + 1)
                st(dve.tensor_scalar(l1v[:, 3:4], l1v[:, 1:2], 1e-12, None, ALU.max))
                st(dve.reciprocal(l1v[:, 4:5], l1v[:, 3:4]))
                st(dve.tensor_scalar(l1v[:, 7:8], l1v[:, 4:5], temp[:, 0:1], 1.0 / N, ALU.mult, ALU.mult))
                e_split(i, 6, 8)
                dve.wait_ge(l1_ps, i * 5 + 3)
                st(dve.scalar_tensor_tensor(out=gram0[:, 0:C], in0=small_ps[0:C, 0:C], scalar=l1v[:, 7:8], in1=negmask,
                                            op0=ALU.mult, op1=ALU.add))
                st(dve.tensor_reduce(l1v[:, 5:6], gram0[:, 0:C], AX.X, ALU.max, negate=True))
                e_split(i, 8, 16)
                dve.wait_ge(l1_exp, i + 1)
                st(dve.reciprocal(l1v[:, 8:9], l1v[:, 6:7]))
                st(dve.tensor_scalar(att_f[:], junk[:], l1v[:, 8:9], None, ALU.mult))
                e_split(i, 16, 20)
                dve.wait_ge(l1_ps, i * 5 + 4)
                st(dve.tensor_tensor(bk[:], small_ps[0:C, None, 0:C].broadcast_to([C, 9, C]),
                                     wk3[:, :, None].broadcast_to([C, 9, C]), ALU.mult))
                e_split(i, 20, U_E)
                dve.wait_ge(stage_evac, (i + 1) * (USES - U_MAX))
                st(dve.tensor_reduce(l1v[:, 9:10], zq[:], AX.X, ALU.add))
                st(dve.reciprocal(l1v[:, 10:11], l1v[:, 9:10]))
                st(dve.tensor_tensor(l1v[:, 11:12], l1v[:, 10:11], l1v[:, 2:3], ALU.mult))
                dve.wait_ge(l1_ps, i * 5 + 5)
                st(dve.tensor_scalar(a32[:].rearrange("p t c -> p (t c)").rearrange("p (s n) -> p s n", s=2),
                                     a_ps[0:C, :, 0:9 * C // 2], l1v[:, 11:12], None, ALU.mult))
                dve.wait_ge(a_hi_ready, i + 1)
                st(dve.tensor_tensor(a_lo[:], a32[:], a_hi[:].bitcast(F32), ALU.subtract))

            def final_sum(i, j):
                s, n = res_use(i, j, True)
                dve.wait_ge(fin_ready, i * NG + j + 1)
                dve.wait_ge(res_loaded[s], n)
                r = res[:, s].rearrange("p (h n) -> p h n", h=2)
                dve.tensor_tensor(r, conv_ps[0:C, j % 2, :, 0:TR * W], r, ALU.add).then_inc(out_done, 1)

            def x1_sum(b, j):
                s, n = res_use(b, j, False)
                dve.wait_ge(conv_ready, b * NG + j + 1)
                dve.wait_ge(res_loaded[s], n)
                dst = x1[0:C, j * GR * W:(j + 1) * GR * W].rearrange("p (h n) -> p h n", h=2)
                dve.tensor_tensor(dst, conv_ps[0:C, j % 2, :, 0:TR * W], res[:, s].rearrange("p (h n) -> p h n", h=2),
                                  ALU.add).then_inc(x1_done, 1)
                dve.wait_ge(x1_done, b * NG + j + 1)
                for k in range(2):
                    dve.bn_stats(stat[:, 2 * j + k, :], dst[:, k, :]).then_inc(x1_stat, 1)

            def attention(b):
                st = small_chain(dve, l0_small, L0_SMALL, b)
                dve.wait_ge(squared, (b + 1) * DIRS * NCH)
                st(dve.tensor_reduce(l0v[:, 8:12], sq[:], AX.X, ALU.add))
                st(dve.tensor_scalar(l0v[:, 0:4], l0v[:, 8:12], 1.0 / N, None, ALU.mult))
                dve.wait_ge(l0_ps, 2 * b + 1)
                st(dve.tensor_copy(hid[:, 0:1], small_ps[0:MID, 504:505]))
                st(dve.scalar_tensor_tensor(out=hid[:, 1:2], in0=hid[:, 0:1], scalar=0.2, in1=hid[:, 0:1],
                                            op0=ALU.mult, op1=ALU.max))
                dve.wait_ge(l0_ps, 2 * b + 2)
                st(dve.tensor_copy(l0v[:, 4:8], small_ps[0:C, 506:510]))
                st(dve.tensor_reduce(l0v[:, 16:17], l0v[:, 4:8], AX.X, ALU.max, negate=True))
                dve.wait_ge(l0_exp, b + 1)
                st(dve.reciprocal(l0v[:, 18:19], l0v[:, 17:18]))
                st(dve.tensor_scalar(l0v[:, 8:12], l0v[:, 12:16], l0v[:, 18:19], None, ALU.mult))

            def combine(b, ch, second):
                flat = acc[:].rearrange("p r c -> p (r c)")
                if ch >= 1:
                    dve.wait_ge(fg_ready, b * NCH + ch)
                for d in range(DIRS):
                    s, v = combo_loaded(b, ch, d)
                    dve.wait_ge(s, v)
                    if d == 0:
                        ins = dve.tensor_scalar(flat, feat[:, 0], l0v[:, 8:9], None, ALU.mult)
                    else:
                        dve.wait_ge(combo, (b * NCH + ch) * DIRS + d)
                        ins = dve.scalar_tensor_tensor(out=flat, in0=feat[:, d], scalar=l0v[:, 8 + d:9 + d], in1=flat,
                                                       op0=ALU.mult, op1=ALU.add)
                    if d == DIRS - 1 and second:
                        dve.wait_ge(fin_ready, (b - 1) * NG + min(NG, 2 * ch + 3))
                    if d == DIRS - 1 and not second and ch == 0:
                        dve.wait_ge(pads_zero, PADS)
                    ins.then_inc(combo, 1)
                dve.wait_ge(fg_hi, b * NCH + ch + 1)
                dve.tensor_tensor(rows(e_lo, ch * CR, CR), acc[:], rows(e_hi, ch * CR, CR).bitcast(F32),
                                  ALU.subtract).then_inc(fg_ready, 1)

            def step(b, first, second):
                i = b - 1
                edge[0] = 0
                if second:
                    chain = small_chain(dve, l1_small, L1_SMALL, i)
                for n in range(STATS):
                    if second:
                        maxes(i, 2 * n, 2 * n + 2)
                    if first:
                        x_stats(b, n, n + 1)
                if second:
                    dve.wait_ge(max_part, (i + 1) * U_MAX)
                    chain(dve.tensor_reduce(nmax[:], mx[:], AX.X, ALU.max, negate=True))
                if first:
                    group_norm(b, STATS, gnx_small, gnx_ps, gnx_pow, 0, xpar, x_stat, (b + 1) * STATS)
                    for ch in range(3):
                        taps(b, ch, 0)
                        taps(b, ch, 1)
                if second:
                    attention_weights(i, chain)
                fin = [0]

                def hook():
                    if second and fin[0] < NG:
                        final_sum(i, fin[0])
                        fin[0] += 1
                if first:
                    for ch in range(3, NCH):
                        taps(b, ch, 0, hook)
                        taps(b, ch, 1, hook)
                while second and fin[0] < NG:
                    hook()
                if first:
                    attention(b)
                    done = 0
                    for ch in range(NCH):
                        combine(b, ch, second)
                        if ch >= 2:
                            x1_sum(b, done)
                            done += 1
                    for j in range(done, NG):
                        x1_sum(b, j)
                    group_norm(b, 2 * NG, gnx1_small, gnx1_ps, gnx1_pow, 2, x1par, x1_stat, (b + 1) * 2 * NG)
            steps(dve, step)

        @block.tensor
        def _(pe):
            pe.wait_ge(w_loaded, 24 * 16)
            pe.matmul(small_ps[0:C, 0:C], m_b[:], s_t[:], start=True, stop=True).then_inc(wc_ready, 1)
            pe.wait_ge(wc_copied, 1)
            pe.wait_ge(wp_ready, 1)
            pe.wait_ge(consts_set, 5)

            def stage(i, u):
                v = u - SLOTS
                if v < 0:
                    pass
                elif v < U_MAX:
                    pe.wait_ge(max_part, i * U_MAX + v + 1)
                else:
                    pe.wait_ge(stage_evac, i * (USES - U_MAX) + v - U_MAX + 1)
                return stage_ps[:, u % SLOTS]

            def evacuated(i, u):
                pe.wait_ge(stage_evac, i * (USES - U_MAX) + u - U_MAX + 1)

            def group_sums(b, chain, done):
                pe.wait_ge(chain, b * GN_SMALL + 2)
                pe.matmul(small_ps[0:C, 500:502], group, mv[:], start=True, stop=True).then_inc(done, 1)

            def conv(i, whi, wlo, done, ready):
                for j in range(NG):
                    ready(j)
                    for h in range(2):
                        r0 = j * GR + h * TR
                        dst = conv_ps[0:C, j % 2, h, 0:TR * W]
                        for t in range(9):
                            dy, dx = t // 3 - 1, t % 3 - 1
                            hi, lo = rows(e_hi, r0 + dy, TR, dx), rows(e_lo, r0 + dy, TR, dx)
                            pe.matmul(dst, whi[:, t, :], hi, start=(t == 0), stop=False)
                            pe.matmul(dst, whi[:, t, :], lo, start=False, stop=False)
                            last = pe.matmul(dst, wlo[:, t, :], hi, start=False, stop=(t == 8))
                    last.then_inc(done, 1)

            def maxes(i):
                for n in range(U_MAX):
                    t = n // 2
                    pe.wait_ge(xn_ready, i * 4 + min(4, (t * BANK + BANK - 1) // (N // 4) + 1))
                    ps = stage(i, n)
                    w = wkv[0:C, 0:C] if n % 2 == 0 else wq
                    pe.matmul(ps[0:C, :], w, x1[0:C, t * BANK:(t + 1) * BANK], start=True, stop=True)\
                        .then_inc(stage_full, 1)

            def dft(i, at):
                for n, (kind, g) in enumerate(DFT_ORDER):
                    ps = stage(i, at + n)
                    if kind == 1:
                        if g == 0:
                            evacuated(i, at - 1)
                        for c in range(4):
                            last = pe.matmul(ps[0:H, c * W:(c + 1) * W], z[:, :, 4 * g + c], w_dft, start=(c == 0), stop=(c == 3),
                                             skip_group_check=True)
                    else:
                        first_of = [k for k, v in enumerate(DFT_ORDER) if v == (1, 2 * g + 1)][0]
                        evacuated(i, at + first_of)
                        d = ps[0:H, 0:8 * NV].rearrange("p (c v) -> p c v", v=NV)
                        pe.matmul(d, dcos, s1[:, g % 2, :, 0:NV], start=True, stop=False)
                        last = pe.matmul(d[:, :, 1:NV - 1], dnsin, s1[:, g % 2, :, NV:W], start=False, stop=True)
                    last.then_inc(stage_full, 1)

            def ctx_rows(i, g):
                evacuated(i, AT_KV + g)
                for r in range(2):
                    last = pe.matmul(ctx_ps[0:C, 0:C], vrow[:, g % 4, r, :], z[:, 2 * g + r, :],
                                     start=(g == 0 and r == 0), stop=(g == U_KV - 1 and r == 1))
                return last

            def q_tiles(i, t0, t1):
                for t in range(t0, t1):
                    ps = stage(i, AT_E + t)
                    pe.matmul(ps[0:C, 0:TR * W], wq, x1[0:C, t * TR * W:(t + 1) * TR * W], start=True, stop=True)\
                        .then_inc(stage_full, 1)

            def attention_block(i, first):
                maxes(i)
                pe.wait_ge(l1_small, i * L1_SMALL + 1)
                pe.matmul(small_ps[0:1, 0:C], nmax[:, 0:1], ident, start=True, stop=True).then_inc(l1_ps, 1)
                if first is not None:
                    pe.wait_ge(maxrow_ready, i + 1)
                    group_sums(first, gnx_small, gnx_ps)
                for g in range(U_ROWS):
                    ps = stage(i, AT_ROWS + g)
                    for r in range(TR):
                        h = g * TR + r
                        last = pe.matmul(ps[0:W, r * C:(r + 1) * C], x1[0:C, h * W:(h + 1) * W], wq1,
                                         start=(r == 0), stop=(r == TR - 1), skip_group_check=True)
                    last.then_inc(stage_full, 1)
                dft(i, AT_DFT1)
                pe.wait_ge(maxrow_ready, i + 1)
                wait(pe, x1_done, (i + 1) * NG)
                for g in range(U_KV + 2):
                    if g < U_KV:
                        ps = stage(i, AT_KV + g)
                        for r in range(2):
                            h = 2 * g + r
                            last = pe.matmul(ps[0:W, r * 2 * C:(r + 1) * 2 * C], x1[:, h * W:(h + 1) * W], wkv[:],
                                             start=(r == 0), stop=(r == 1), skip_group_check=True)
                        last.then_inc(stage_full, 1)
                    if g >= 2:
                        ctx_rows(i, g - 2)
                dft(i, AT_DFT2)
                evacuated(i, AT_DFT2 + U_DFT - 1)
                for v in (0, NV - 1):
                    pe.matmul(gram_ps[0:C, 0:2 * C], t_sp[:, v, 0:C], t_sp[:, v, :], start=(v == 0), stop=(v != 0))
                for v in range(1, NV - 1):
                    pe.matmul(gram_ps[0:C, 2 * C:4 * C], t_sp[:, v, 0:C], t_sp[:, v, :], start=(v == 1), stop=(v == NV - 2))
                pe.matmul(small_ps[0:C, 2 * C:2 * C + 1], t_sp[0:1, 0, C:2 * C], one[0:1, 0:1], start=True, stop=True)\
                    .then_inc(gram_done, 1)
                q_tiles(i, 0, 6)
                pe.wait_ge(l1_small, i * L1_SMALL + 4)
                pe.matmul(small_ps[0:C, 0:C], wq2t, gram[:, 0:C], start=True, stop=True)
                pe.matmul(small_ps[0:C, C:2 * C], gram[:, C:2 * C], wq2t, start=True, stop=True)
                pe.matmul(ctx_ps[0:C, 128:128 + C], wc[:], ctxm[:], start=True, stop=True).then_inc(l1_ps, 1)
                q_tiles(i, 6, 8)
                pe.wait_ge(l1_small, i * L1_SMALL + 7)
                pe.matmul(small_ps[0:C, 0:C], s_t[:], ident, start=True, stop=True).then_inc(l1_ps, 1)
                q_tiles(i, 8, 16)
                pe.wait_ge(l1_small, i * L1_SMALL + 15)
                pe.matmul(small_ps[0:C, 0:C], att_f[:], wpft, start=True, stop=True).then_inc(l1_ps, 1)
                q_tiles(i, 16, U_E)
                pe.wait_ge(l1_small, i * L1_SMALL + 16)
                flat = bk[:].rearrange("p t c -> p (t c)")
                half = 9 * C // 2
                pe.matmul(a_ps[0:C, 0, 0:half], m_b[:], flat[:, 0:half], start=True, stop=True)
                pe.matmul(a_ps[0:C, 1, 0:half], m_b[:], flat[:, half:2 * half], start=True, stop=True).then_inc(l1_ps, 1)

                def ready(j):
                    if j == 0:
                        pe.wait_ge(l1_small, i * L1_SMALL + 21)
                        pe.wait_ge(e_ready, (i + 1) * U_E)
                    elif j >= 2:
                        pe.wait_ge(out_done, i * NG + j - 1)
                conv(i, a_hi, a_lo, fin_ready, ready)

            def step(b, first, second):
                if second:
                    attention_block(b - 1, b if first else None)
                elif first:
                    group_sums(b, gnx_small, gnx_ps)
                if first:
                    pe.wait_ge(l0_small, b * L0_SMALL + 2)
                    for d in range(DIRS):
                        last = pe.matmul(small_ps[0:MID, 504:505], att1[:, d, :], l0v[:, d:d + 1], start=(d == 0),
                                         stop=(d == DIRS - 1))
                    last.then_inc(l0_ps, 1)
                    pe.wait_ge(l0_small, b * L0_SMALL + 4)
                    for d in range(DIRS):
                        last = pe.matmul(small_ps[0:C, 506 + d:507 + d], att2[:, d * C:(d + 1) * C], hid[:, 1:2],
                                         start=True, stop=True)
                    last.then_inc(l0_ps, 1)

                    def ready(j):
                        pe.wait_ge(fg_ready, b * NCH + min(NCH - 1, (j + 1) * GR // CR) + 1)
                        if j < 2:
                            if second:
                                pe.wait_ge(out_done, (b - 1) * NG + NG - 1 + j)
                        else:
                            pe.wait_ge(x1_done, b * NG + j - 1)
                    conv(b, wp_hi, wp_lo, conv_ready, ready)
                    group_sums(b, gnx1_small, gnx1_ps)
            steps(pe, step)


NAMES = ["x", "ident", "group", "mask", "negmask", "w_dft", "dcos", "dnsin", "wq", "wq1", "wq2", "wq2t", "wpft",
         "wkv", "wh", "wv", "w45", "w135", "wk3", "temp", "att1", "att2", "wp", "w_mid", "wkvv"]


def kernel(x, L0_conv_w_h, L0_conv_w_v, L0_conv_w_d45, L0_conv_w_d135, L0_conv_w_att1, L0_conv_w_att2,
           L0_conv_w_proj, L1_conv_temperature, L1_conv_w_qkv, L1_conv_w_proj, L1_conv_w_kv, L1_conv_w_q1,
           L1_conv_w_q2, L1_conv_w_kvconv, L1_conv_w_projf):
    import numpy as np
    import concourse.bacc as bacc
    from concourse.bass_utils import run_bass_kernel_spmd

    f = np.float32
    n = np.arange(W)
    angle = 2 * np.pi * np.outer(n, n) / W
    cos, sin = np.cos(angle), np.sin(angle)
    head = n // HD
    same = head[:, None] == head[None, :]
    grp = n // 3
    qkv = np.asarray(L1_conv_w_qkv)
    t = {
        "x": np.asarray(x).reshape(B, C, N),
        "ident": np.eye(C).astype(f),
        "group": ((grp[:, None] == grp[None, :]) / 3.0).astype(f),
        "mask": same.astype(f),
        "negmask": np.where(same, 0.0, -1e30).astype(f),
        "w_dft": np.concatenate([cos[:, :NV], sin[:, 1:NV - 1]], 1).astype(f),
        "dcos": cos.astype(f),
        "dnsin": (-sin).astype(f),
        "wq": qkv[0:C].T, "wkv": qkv[C:3 * C].T,
        "wq1": np.asarray(L1_conv_w_q1).T, "wq2": np.asarray(L1_conv_w_q2), "wq2t": np.asarray(L1_conv_w_q2).T,
        "wpft": np.asarray(L1_conv_w_projf).T,
        "wh": np.asarray(L0_conv_w_h).reshape(C, KT), "wv": np.asarray(L0_conv_w_v).reshape(C, KT),
        "w45": np.asarray(L0_conv_w_d45).reshape(C, KT * KT), "w135": np.asarray(L0_conv_w_d135).reshape(C, KT * KT),
        "wk3": np.asarray(L1_conv_w_kvconv)[C:].reshape(C, 9),
        "temp": np.repeat(np.asarray(L1_conv_temperature).reshape(HEADS, 1), HD, 0),
        "att1": np.asarray(L0_conv_w_att1).reshape(MID, DIRS, C).transpose(2, 1, 0),
        "att2": np.asarray(L0_conv_w_att2).T,
        "wp": np.asarray(L0_conv_w_proj).transpose(1, 2, 3, 0).reshape(C, 9, C),
        "w_mid": np.asarray(L1_conv_w_proj),
        "wkvv": np.asarray(L1_conv_w_kv)[C:].T,
    }
    nc = bacc.Bacc("TRN2", target_bir_lowering=False, num_devices=1)
    arrays, aps = {}, {}
    for name in NAMES:
        arrays["in_" + name] = np.ascontiguousarray(t[name])
        aps[name] = nc.dram_tensor("in_" + name, arrays["in_" + name].shape, F32, kind="ExternalInput").ap()
    out = nc.dram_tensor("out", (B, C, N), F32, kind="ExternalOutput").ap()
    build(nc, aps, out)
    r = run_bass_kernel_spmd(nc, [arrays], core_ids=[0])
    return r.results[0]["out"].reshape(B, C, H, W)
```

```python
from contextlib import ExitStack

import concourse.bass as bass
from concourse import mybir

F32 = mybir.dt.float32
F32R = mybir.dt.float32r
ALU = mybir.AluOpType
ACT = mybir.ActivationFunctionType
AX = mybir.AxisListType

B, C, H, W = 8, 96, 96, 96
N = H * W
HEADS, HD = 4, 24
MID = 48
DIRS, KT = 4, 7
PAD = KT // 2
CR = 16
NCH = H // CR
XR, XP = CR + 2 * PAD, W + 2 * PAD
GR = 8
NG = H // GR
TR = 4
EP = W + 1
EN = (H + 2) * EP + 2
NV = W // 2 + 1
BANK = 512
SLOTS = 5
RES = 3
STATS = N // BANK
XSTAT = CR * W // BANK

U_MAX = 2 * STATS
U_ROWS = H // TR
U_DFT = C // 4 + C // 8
U_KV = H // 2
U_E = H // TR
AT_ROWS = U_MAX
AT_DFT1 = AT_ROWS + U_ROWS
AT_KV = AT_DFT1 + U_DFT
AT_DFT2 = AT_KV + U_KV
AT_E = AT_DFT2 + U_DFT
USES = AT_E + U_E

DFT_ORDER = []
for _j in range(C // 8 + 1):
    if _j < C // 8:
        DFT_ORDER += [(1, 2 * _j), (1, 2 * _j + 1)]
    if _j >= 1:
        DFT_ORDER.append((2, _j - 1))
assert len(DFT_ORDER) == U_DFT

CENTRE_FIRST = (4, 0, 1, 2, 3, 5, 6, 7, 8)
CENTRE_LAST = CENTRE_FIRST[::-1]
PADS = 6
TAPS = DIRS * (KT - 1)
UNITS = 2 * NCH
LEAD = 8
LEAD_TAPS = TAPS // 2
EARLY_TAPS = 8
MAX_TAPS = TAPS // 2 - EARLY_TAPS
UNIT_USES, UNIT_AT = 20, AT_ROWS + 8
assert UNIT_AT + (LEAD - 2) * UNIT_USES <= AT_E
SUMS_AFTER = (0, 0, 0, 1, 1, 1)
GN_AT = sum(SUMS_AFTER) + 2
HID_AT = 7
EDGES = 2
XN = STATS
ETILES = 3
VROWS, BEHIND = 4, 3
L0_SMALL, L1_SMALL, GN_SMALL = 8, 21, 7


def unit(u):
    return u // 2, NCH - 1 - u // 2, (u % 2 * 2, u % 2 * 2 + 1)


def first_image(b):
    return isinstance(b, int) and b == 0


def taps_before(b):
    return 0 if first_image(b) else b * (NCH * TAPS) - NCH * (KT - 1)


def unit_taps(b, u, k, parity):
    if first_image(b) and u % 2:
        return taps_before(b) + u // 2 * (TAPS - (KT - 1)) + TAPS // 2 + k
    per_turn = TAPS - (KT - 1) if first_image(b) else TAPS
    return taps_before(b) + u // 2 * per_turn + u % 2 * (TAPS // 2) + 2 * (k - 1) + parity + 1


def firsts_before(b, q):
    return q * (DIRS - 1) if first_image(b) else b * (DIRS * NCH) - NCH + q * DIRS


def tap_shift(d, k):
    s = k - PAD
    return [(0, s), (s, 0), (s, s), (s, -s)][d]


def build(nc, a, out):
    with ExitStack() as ctx:
        def sb(name, shape, dt=F32):
            return ctx.enter_context(nc.sbuf_tensor(name, shape, dt))

        def sem(name):
            return ctx.enter_context(nc.semaphore(name))

        EBYTES = -(-EN * 4 // 32) * 32
        arena = sb("arena", [128, 2 * EBYTES // 4])
        lo0 = nc.sbuf_base - 2 * EBYTES
        e_hi = nc.alloc_sbuf_tensor_at("e_hi", [C, EN], F32R, offset=lo0)
        e_lo = nc.alloc_sbuf_tensor_at("e_lo", [C, EN], F32R, offset=lo0 + EBYTES)
        z = nc.alloc_sbuf_tensor_at("z", [W, H, C], F32, offset=lo0)
        t_sp = nc.alloc_sbuf_tensor_at("t_sp", [H, NV, 2 * C], F32, offset=lo0 + H * C * 4)
        assert (H * C + NV * 2 * C) * 4 <= 2 * EBYTES
        SBYTES = CR * W * 4
        arena2 = sb("arena2", [128, SBYTES // 4])
        s0 = nc.sbuf_base - SBYTES
        s1 = nc.alloc_sbuf_tensor_at("s1", [H, 2, 8, W], F32, offset=s0)
        a32 = nc.alloc_sbuf_tensor_at("a32", [C, 9, C], F32, offset=s0)
        acc = nc.alloc_sbuf_tensor_at("acc", [C, CR, W], F32, offset=s0)

        x1 = sb("x1", [C + 1, N])
        xin = sb("xin", [C, 2, XR, XP])
        feat = sb("feat", [C, DIRS, CR * W])
        res = sb("res", [C, RES, GR * W])
        vrow = sb("vrow", [W, VROWS, 2, C])
        etile = sb("etile", [C, ETILES, TR * W])
        wp_hi, wp_lo = sb("wp_hi", [C, 9, C], F32R), sb("wp_lo", [C, 9, C], F32R)
        a_hi, a_lo = sb("a_hi", [C, 9, C], F32R), sb("a_lo", [C, 9, C], F32R)
        bk = sb("bk", [C, 9, C])
        wkv = sb("wkv", [C + 1, 2 * C])
        mats = sb("mats", [C, 12, C])
        ident, group, mask, negmask, w_dft, dcos, dnsin, wq, wq1, wq2, wq2t, wpft = (
            mats[:, i, :] for i in range(12))
        wc = sb("wc", [C, C])
        wh, wv = sb("wh", [C, KT]), sb("wv", [C, KT])
        w45, w135 = sb("w45", [C, KT * KT]), sb("w135", [C, KT * KT])
        wk3, temp = sb("wk3", [C, 9]), sb("temp", [C, 1])
        att1, att2 = sb("att1", [C, DIRS, MID]), sb("att2", [MID, DIRS * C])
        xstats, x1stats = sb("xstats", [C, STATS, 6]), sb("x1stats", [C, 2 * NG, 6])
        mv, gstat, gpar = sb("mv", [C, 2]), sb("gstat", [C, 2]), sb("gpar", [C, 4])
        xpar, x1par = sb("xpar", [C, 2]), sb("x1par", [C, 2])
        consts = sb("consts", [C, 2])
        one = sb("one", [C, 1])
        sq = sb("sq", [C, DIRS, NCH])
        sqjunk = sb("sqjunk", [C, CR * W], mybir.dt.bfloat16)
        l0v = sb("l0v", [C, 20])
        hid = sb("hid", [MID, 2])
        mx = sb("mx", [C, 2, STATS])
        nmax = sb("nmax", [C, 2])
        zq = sb("zq", [C, U_E])
        l1v = sb("l1v", [C, 16])
        gram, gram0 = sb("gram", [C, 2 * C]), sb("gram0", [C, 2 * C])
        ctxm, s_t, m_b, att_f, junk = (sb(n, [C, C]) for n in ("ctxm", "s_t", "m_b", "att_f", "junk"))

        banks = ctx.enter_context(nc.psum_tensor("banks", [128, 8, BANK], F32))
        conv_ps = banks[:, 0:4].rearrange("p (s h) n -> p s h n", s=2)
        stage_ps, small_ps = banks[:, 2:2 + SLOTS], banks[:, 7]
        ctx_ps, gram_ps, a_ps = banks[:, 0], banks[:, 1], banks[:, 0:2]

        feats_d = nc.dram_tensor("feats_d", (DIRS, C, N), F32, kind="Internal").ap()

        w_loaded = sem("w_loaded")
        xin_loaded = [sem(f"xin_loaded{i}") for i in range(2)]
        feat_loaded = [sem(f"feat_loaded{i}") for i in range(DIRS)]
        feat_stored = [sem(f"feat_stored{i}") for i in range(DIRS)]
        res_loaded = [sem(f"res_loaded{i}") for i in range(RES)]
        out_stored = [sem(f"out_stored{i}") for i in range(RES)]
        x1_stored = sem("x1_stored")
        zeroed, consts_set, wc_ready, wc_copied, wp_hi_ready, wp_ready = map(sem, (
            "zeroed", "consts_set", "wc_ready", "wc_copied", "wp_hi_ready", "wp_ready"))
        x_stat = sem("x_stat")
        gnx_small, gnx1_small = sem("gnx_small"), sem("gnx1_small")
        gnx_ps, gnx1_ps = sem("gnx_ps"), sem("gnx1_ps")
        gnx_pow, gnx1_pow = sem("gnx_pow"), sem("gnx1_pow")
        xin_ready = sem("xin_ready")
        edge_zero = sem("edge_zero")
        tap_first = sem("tap_first")
        tap_done = sem("tap_done")
        last_dir_sums, last_dir_made = sem("last_dir_sums"), sem("last_dir_made")
        diag_ready = sem("diag_ready")
        squared = sem("squared")
        l0_small, l0_ps, l0_exp = sem("l0_small"), sem("l0_ps"), sem("l0_exp")
        combo = sem("combo")
        fg_hi, fg_ready = sem("fg_hi"), sem("fg_ready")
        conv_ready = sem("conv_ready")
        x1_done, x1_stat = sem("x1_done"), sem("x1_stat")
        xn_ready = sem("xn_ready")
        stage_full = sem("stage_full")
        max_part = sem("max_part")
        stage_evac = sem("stage_evac")
        l1_small, l1_ps = sem("l1_small"), sem("l1_ps")
        maxrow_ready, gram_done, l1_pow, l1_exp = map(sem, ("maxrow_ready", "gram_done", "l1_pow", "l1_exp"))
        pads_zero, e_hi_ready, e_ready, a_hi_ready = map(sem, ("pads_zero", "e_hi_ready", "e_ready", "a_hi_ready"))
        fin_ready, fin_copied = sem("fin_ready"), sem("fin_copied")
        waits_passed = {e.engine: sem(n) for e, n in (
            (nc.sync, "sp_passed"), (nc.gpsimd, "pool_passed"), (nc.vector, "dve_passed"))}

        block = ctx.enter_context(nc.Block())

        def wait(eng, s, value):
            if not isinstance(value, int) or value > 0:
                eng.wait_ge(s, value)

        def apart(eng):
            eng.sem_inc(waits_passed[eng.engine], 1)

        def rows(buf, r0, n, dx=0):
            at = (r0 + 1) * EP + 1 + dx
            return buf[:, at:at + n * EP].rearrange("p (r c) -> p r c", c=EP)[:, :, 0:W]

        def small_chain(eng, s, total, i):
            state = [0]

            def step(ins):
                state[0] += 1
                assert state[0] <= total
                ins.then_inc(s, 1)
                eng.wait_ge(s, i * total + state[0])
            return step

        def stat_slot(n):
            return (n + NCH) % DIRS

        nstat = [len([n for n in range(NCH) if stat_slot(n) == s]) for s in range(DIRS)]
        per_slot = [nstat[s] + NCH - 1 for s in range(DIRS)]

        def stat_loaded(b, n):
            s = stat_slot(n)
            return feat_loaded[s], (b * per_slot[s] + n // DIRS + 1) * 16

        def summed(ch, k):
            return (ch + k) % DIRS

        def slot_free(b, ch, k):
            return (b * NCH + ch - 1) * DIRS + min(k + 2, DIRS)

        def combo_loaded(b, ch, d):
            return feat_loaded[d], (b * per_slot[d] + nstat[d] + ch) * 16

        def res_loads(b, j):
            return res_loaded[j % RES], (b * (NG // RES) + j // RES + 1) * 16

        def image(t, i):
            return t[i] if isinstance(i, int) else t[bass.ds(i, 1)].rearrange("a c n -> (a c) n")

        def steps(eng, start, step):
            start(0)
            step(0, True, False, True)
            with eng.Fori(1, B - 1) as b:
                step(b, True, True, True)
            step(B - 1, True, True, False)
            step(B, False, True, False)

        @block.sync
        def _(sp):
            loads = [(mats[:, n, :], a[k]) for n, k in enumerate(
                ("ident", "group", "mask", "negmask", "w_dft", "dcos", "dnsin", "wq", "wq1", "wq2", "wq2t", "wpft"))]
            loads += [(wkv[0:C, :], a["wkv"]), (wh[:], a["wh"]), (wv[:], a["wv"]), (w45[:], a["w45"]),
                      (w135[:], a["w135"]), (wk3[:], a["wk3"]), (temp[:], a["temp"]), (att1[:], a["att1"]),
                      (att2[:], a["att2"]), (a32[:], a["wp"]), (m_b[:], a["w_mid"]), (s_t[:], a["wkvv"])]
            def load_xin(b, q):
                ch = NCH - 1 - q
                lo, hi = max(0, ch * CR - PAD), min(H, ch * CR + CR + PAD)
                at = lo - (ch * CR - PAD)
                x = image(a["x"], b)
                if q >= 2:
                    wait(sp, tap_done, unit_taps(b, 2 * q - 3, KT - 1, 0 if first_image(b) else 1))
                else:
                    last_turn = TAPS - (KT - 1) if isinstance(b, int) and b == 1 else TAPS
                    wait(sp, tap_done, 0 if first_image(b) else taps_before(b) + (q - 1) * last_turn)
                if first_image(b) and q >= 2:
                    sp.wait_ge(last_dir_sums, 2 * (q - 1))
                apart(sp)
                if isinstance(b, int) and b == 1:
                    sp.wait_ge(last_dir_sums, 2 * NCH)
                if isinstance(b, int) and b == 0 and q < 2:
                    sp.wait_ge(zeroed, 1)
                sp.dma_start(xin[:, q % 2, at:at + hi - lo, PAD:PAD + W],
                             x[:, lo * W:hi * W].rearrange("c (r w) -> c r w", w=W)).then_inc(xin_loaded[q % 2], 16)

            def start(b):
                x = image(a["x"], b)
                for n in range(NCH):
                    s = stat_slot(n)
                    if n < DIRS:
                        wait(sp, combo, slot_free(b, 0, n))
                    else:
                        wait(sp, x_stat, b * STATS + (n - DIRS + 1) * XSTAT)
                    sp.dma_start(feat[:, s], x[:, n * CR * W:(n + 1) * CR * W]).then_inc(feat_loaded[s], 16)
                    if first_image(b) and n == 1:
                        for dst, src in loads:
                            sp.dma_start(dst, src).then_inc(w_loaded, 16)
                load_xin(b, 0)
                load_xin(b, 1)

            def step(b, first, second, more):
                if not first:
                    return
                for u in range(UNITS - 2):
                    q, ch, dirs = unit(u)
                    for d in dirs:
                        if first_image(b) and d == DIRS - 1:
                            sp.wait_ge(last_dir_made, 2 * (q + 1))
                        else:
                            wait(sp, tap_done, unit_taps(b, u, KT - 1, d % 2))
                        sp.dma_start(feats_d[d, :, ch * CR * W:(ch + 1) * CR * W], feat[:, d]).then_inc(feat_stored[d], 16)
                    if u % 2 and q + 2 < NCH:
                        load_xin(b, q + 2)
                for ch in range(1, NCH):
                    for k in range(DIRS):
                        d = summed(ch, k)
                        if ch == 1:
                            wait(sp, feat_stored[d], (b + 1) * (NCH - 1) * 16)
                            apart(sp)
                        wait(sp, combo, slot_free(b, ch, k))
                        sp.dma_start(feat[:, d], feats_d[d, :, ch * CR * W:(ch + 1) * CR * W]).then_inc(feat_loaded[d], 16)
                if more:
                    start(b + 1)
            steps(sp, start, step)

        @block.gpsimd
        def _(pool):
            def gn_pow(chain, per, i, at, col, done):
                wait(pool, chain, i * per + at)
                pool.tensor_tensor(gpar[:, col:col + 1], gpar[:, col:col + 1], consts[:, 0:1], ALU.pow).then_inc(done, 1)

            def zero_pads():
                for e in (e_hi, e_lo):
                    f = e[:, :].bitcast(F32)
                    pool.memset(f[:, 0:EP], 0.0).then_inc(pads_zero, 1)
                    pool.memset(f[:, (H + 1) * EP:EN], 0.0).then_inc(pads_zero, 1)
                    pool.memset(f[:, EP:EP + H * EP].rearrange("p (r c) -> p r c", c=EP)[:, :, 0:1], 0.0)\
                        .then_inc(pads_zero, 1)

            def start(b):
                gn_pow(gnx_small, GN_SMALL, b, 5, 0, gnx_pow)

            def step(b, first, second, more):
                if second:
                    i = b - 1
                    pool.wait_ge(gram_done, i + 1)
                    apart(pool)
                    zero_pads()
                    pool.wait_ge(l1_small, i * L1_SMALL + 5)
                    pool.tensor_tensor(l1v[:, 1:2], l1v[:, 0:1], consts[:, 1:2], ALU.pow).then_inc(l1_pow, 1)
                    o = image(out, i)
                    for j in range(NG):
                        pool.wait_ge(fin_copied, i * NG + j + 1)
                        if j == 0:
                            apart(pool)
                            pool.wait_ge(x1_stored, (i + 1) * NG * 16)
                        apart(pool)
                        pool.dma_start(o[:, j * GR * W:(j + 1) * GR * W], res[:, j % RES], accum_op=ALU.add)\
                            .then_inc(out_stored[j % RES], 16)
                if first:
                    if not second:
                        zero_pads()
                    x, o = image(a["x"], b), image(out, b)
                    for j in range(NG + 1):
                        if j < NG:
                            if j < RES:
                                wait(pool, out_stored[j], b * (NG // RES) * 16)
                            else:
                                wait(pool, x1_done, b * NG + j - RES + 1)
                            apart(pool)
                            pool.dma_start(res[:, j % RES], x[:, j * GR * W:(j + 1) * GR * W])\
                                .then_inc(res_loaded[j % RES], 16)
                        if j >= 1:
                            pool.wait_ge(x1_done, b * NG + j)
                            apart(pool)
                            pool.dma_start(o[:, (j - 1) * GR * W:j * GR * W], x1[0:C, (j - 1) * GR * W:j * GR * W])\
                                .then_inc(x1_stored, 16)
                        if more and j == GN_AT:
                            start(b + 1)
                    gn_pow(gnx1_small, GN_SMALL, b, 5, 2, gnx1_pow)

            pool.memset(xin[:], 0.0).then_inc(zeroed, 1)
            pool.memset(x1[C:C + 1, :], 1.0).then_inc(consts_set, 1)
            pool.memset(wkv[C:C + 1, C:2 * C], 0.0).then_inc(consts_set, 1)
            pool.memset(one[:], 1.0).then_inc(consts_set, 1)
            pool.memset(consts[:, 0:1], -0.5).then_inc(consts_set, 1)
            pool.memset(consts[:, 1:2], 0.5).then_inc(consts_set, 1)
            pool.wait_ge(consts_set, 5)
            steps(pool, start, step)
            for s in range(RES):
                pool.wait_ge(out_stored[s], B * (NG // RES) * 16)

        @block.scalar
        def _(act):
            wp32 = a32
            beside = [None]
            first_w = [wh[:, 0:1], wv[:, 0:1], w45[:, 0:1], w135[:, KT - 1:KT]]
            act.wait_ge(w_loaded, 24 * 16)
            act.activation(wp_hi[:], wp32[:], ACT.Identity).then_inc(wp_hi_ready, 1)
            act.wait_ge(wc_ready, 1)
            act.activation(wc[:], small_ps[0:C, 0:C], ACT.Identity).then_inc(wc_copied, 1)
            for k in range(KT):
                act.activation(bk[:, k, :], ident, ACT.Identity,
                               scale=w135[:, k * KT + KT - 1 - k:k * KT + KT - k]).then_inc(diag_ready, 1)

            def norm_chunk(b, q):
                ch = NCH - 1 - q
                lo, hi = max(0, ch * CR - PAD), min(H, ch * CR + CR + PAD)
                at = lo - (ch * CR - PAD)
                if q == 0:
                    act.wait_ge(gnx_small, b * GN_SMALL + GN_SMALL)
                act.wait_ge(xin_loaded[q % 2], (b * (NCH // 2) + q // 2 + 1) * 16)
                v = xin[:, q % 2, at:at + hi - lo, PAD:PAD + W]
                act.activation(v, v, ACT.Identity, scale=xpar[:, 0:1], bias=xpar[:, 1:2]).then_inc(xin_ready, 1)

            def first_tap(b, u, d):
                q, ch, dirs = unit(u)
                d = dirs[d]
                dy, dx = tap_shift(d, 0)
                by_pe = first_image(b) and d == DIRS - 1
                act.wait_ge(xin_ready, b * NCH + q + 1)
                if q == NCH - 1:
                    act.wait_ge(edge_zero, (b + 1) * EDGES)
                if q >= 1:
                    act.wait_ge(squared, b * DIRS * NCH + (q - 1) * DIRS + d + 1)
                    act.wait_ge(feat_stored[d], (b * (NCH - 1) + q) * 16)
                if by_pe:
                    for half in range(2):
                        act.wait_ge(last_dir_sums, 2 * q + half + 1)
                        act.activation(feat[:, d].rearrange("p (s h n) -> p s h n", s=2, h=2)[:, half],
                                       conv_ps[0:C, half, :, 0:TR * W], ACT.Identity).then_inc(last_dir_made, 1)
                    return
                act.activation(feat[:, d].rearrange("p (r c) -> p r c", c=W),
                               xin[:, q % 2, PAD + dy:PAD + dy + CR, PAD + dx:PAD + dx + W],
                               ACT.Identity, scale=first_w[d]).then_inc(tap_first, 1)

            def square(b, u, d):
                q, ch, dirs = unit(u)
                d = dirs[d]
                if first_image(b) and d == DIRS - 1:
                    act.wait_ge(last_dir_made, 2 * (q + 1))
                else:
                    act.wait_ge(tap_done, unit_taps(b, u, KT - 1, d % 2))
                wait(act, squared, b * DIRS * NCH + q * DIRS + d)
                act.activation(sqjunk[:], feat[:, d], ACT.Square, accum_out=sq[:, d, ch:ch + 1]).then_inc(squared, 1)

            def unit_work(b, u, part=None):
                work = [(square, u, 0), (square, u, 1)]
                if u in (2, 4, 6, 8):
                    work.append((norm_chunk, u // 2 + 1))
                if u + 2 < UNITS:
                    work += [(first_tap, u + 2, 0), (first_tap, u + 2, 1)]
                for f, *args in work if part is None else work[part:part + 1]:
                    f(b, *args)

            def stage(i, u):
                n, after = divmod(u - UNIT_AT, UNIT_USES)
                if beside[0] is not None and 0 <= n < LEAD - 2 and after % 4 == 0:
                    unit_work(beside[0], n + 1, after // 4)
                act.wait_ge(stage_full, i * USES + u + 1)
                return stage_ps[:, u % SLOTS]

            def max_row(i):
                act.wait_ge(l1_ps, i * 5 + 1)
                act.activation(wkv[C:C + 1, 0:C], small_ps[0:1, 0:C], ACT.Identity).then_inc(maxrow_ready, 1)

            def u_rows(i):
                for g in range(U_ROWS):
                    ps = stage(i, AT_ROWS + g)
                    act.activation(z[:, g * TR:(g + 1) * TR, :], ps[0:W, 0:TR * C].rearrange("p (r c) -> p r c", c=C),
                                   ACT.Identity).then_inc(stage_evac, 1)

            def dft(i, at, ch0, func):
                for n, (kind, g) in enumerate(DFT_ORDER):
                    ps = stage(i, at + n)
                    if kind == 1:
                        act.activation(s1[:, (g // 2) % 2, (g % 2) * 4:(g % 2) * 4 + 4, :],
                                       ps[0:H, 0:4 * W].rearrange("p (c v) -> p c v", v=W), ACT.Identity).then_inc(stage_evac, 1)
                    else:
                        act.activation(t_sp[:, :, ch0 + 8 * g:ch0 + 8 * g + 8].rearrange("p v c -> p c v"),
                                       ps[0:H, 0:8 * NV].rearrange("p (c v) -> p c v", v=NV), func).then_inc(stage_evac, 1)

            def kv_rows(i):
                for g in range(U_KV):
                    ps = stage(i, AT_KV + g)[0:W, 0:4 * C].rearrange("p (r c) -> p r c", c=2 * C)
                    act.activation(z[:, 2 * g:2 * g + 2, :], ps[:, :, 0:C], ACT.Exp)
                    act.activation(vrow[:, g % VROWS], ps[:, :, C:2 * C], ACT.Identity).then_inc(stage_evac, 1)

            def e_tiles(i, t0, t1):
                for t in range(t0, t1):
                    ps = stage(i, AT_E + t)
                    if t == 0:
                        act.wait_ge(pads_zero, (i + 2) * PADS)
                    if t >= ETILES:
                        act.wait_ge(e_ready, i * U_E + t - ETILES + 1)
                    act.activation(etile[:, t % ETILES], ps[0:C, 0:TR * W], ACT.Exp, bias=nmax[:, 1:2],
                                   accum_out=zq[:, t:t + 1]).then_inc(stage_evac, 1)

            def final_copy(i, j):
                act.wait_ge(fin_ready, i * NG + j + 1)
                if j >= RES:
                    act.wait_ge(out_stored[j % RES], (i * (NG // RES) + j // RES) * 16)
                act.activation(res[:, j % RES].rearrange("p (h n) -> p h n", h=2), conv_ps[0:C, j % 2, :, 0:TR * W],
                               ACT.Identity).then_inc(fin_copied, 1)

            def attn_exp(i):
                act.wait_ge(l1_small, i * L1_SMALL + 13)
                act.activation(junk[:], gram0[:, 0:C], ACT.Exp, bias=l1v[:, 5:6], accum_out=l1v[:, 6:7]).then_inc(l1_exp, 1)

            def a_split(i):
                act.wait_ge(l1_small, i * L1_SMALL + 20)
                act.activation(a_hi[:], a32[:], ACT.Identity).then_inc(a_hi_ready, 1)

            def att_softmax(b):
                act.wait_ge(l0_small, b * L0_SMALL + 6)
                act.activation(l0v[:, 12:16], l0v[:, 4:8], ACT.Exp, bias=l0v[:, 16:17], accum_out=l0v[:, 17:18]).then_inc(l0_exp, 1)

            def fg_high(b, ch):
                act.wait_ge(combo, (b * NCH + ch + 1) * DIRS)
                act.activation(rows(e_hi, ch * CR, CR), acc[:], ACT.Identity).then_inc(fg_hi, 1)

            def xn(b):
                act.wait_ge(gnx1_small, b * GN_SMALL + GN_SMALL)
                act.wait_ge(x1_stored, (b + 1) * NG * 16)
                for p in range(XN):
                    v = x1[0:C, p * (N // XN):(p + 1) * (N // XN)]
                    act.activation(v, v, ACT.Identity, scale=x1par[:, 0:1], bias=x1par[:, 1:2]).then_inc(xn_ready, 1)

            def start(b):
                norm_chunk(b, 0)
                norm_chunk(b, 1)
                for u in range(2):
                    first_tap(b, u, 0)
                    first_tap(b, u, 1)
                unit_work(b, 0)

            def step(b, first, second, more):
                i = b - 1
                beside[0] = b if first and second else None
                if second:
                    u_rows(i)
                    max_row(i)
                    dft(i, AT_DFT1, 0, ACT.Gelu)
                    kv_rows(i)
                    dft(i, AT_DFT2, C, ACT.Identity)
                if first:
                    for u in range(LEAD - 1 if second else 1, LEAD + 1):
                        unit_work(b, u)
                if second:
                    e_tiles(i, 0, 9)
                    attn_exp(i)
                    e_tiles(i, 9, U_E)
                    a_split(i)

                def copies(j0, j1):
                    if second:
                        for j in range(j0, j1):
                            final_copy(i, j)
                j = 0
                for u in range(LEAD + 1, UNITS):
                    copies(j, j + 2)
                    j += 2
                    if first:
                        unit_work(b, u)
                copies(j, HID_AT + 1)
                if first:
                    att_softmax(b)
                for ch in range(NCH):
                    copies(min(NG, HID_AT + 1 + ch), min(NG, HID_AT + 2 + ch) if ch < NCH - 1 else NG)
                    if first:
                        fg_high(b, ch)
                if first:
                    if more:
                        start(b + 1)
                    xn(b)
            steps(act, start, step)

        @block.vector
        def _(dve):
            taps_w = [lambda k: wh[:, k:k + 1], lambda k: wv[:, k:k + 1],
                      lambda k: w45[:, k * KT + k:k * KT + k + 1],
                      lambda k: w135[:, k * KT + KT - 1 - k:k * KT + KT - k]]
            def set_up():
                dve.wait_ge(w_loaded, 24 * 16)
                dve.wait_ge(zeroed, 1)
                dve.wait_ge(consts_set, 5)
                dve.wait_ge(wp_hi_ready, 1)
                dve.tensor_tensor(wp_lo[:], a32[:], wp_hi[:].bitcast(F32), ALU.subtract).then_inc(wp_ready, 1)

            def x_stats(b, n0, n1):
                for n in range(n0, n1):
                    ch, k = n // XSTAT, n % XSTAT
                    if k == 0:
                        s, v = stat_loaded(b, ch)
                        dve.wait_ge(s, v)
                    dve.bn_stats(xstats[:, n, :], feat[:, stat_slot(ch), k * BANK:(k + 1) * BANK]).then_inc(x_stat, 1)

            def group_norm(b, stats, chain, ps_sem, pow_sem, col, par, last_stat, last_count):
                st = small_chain(dve, chain, GN_SMALL, b)
                dve.wait_ge(last_stat, last_count)
                apart(dve)
                st(dve.bn_aggr(mv[:], stats[:]))
                st(dve.scalar_tensor_tensor(out=mv[:, 1:2], in0=mv[:, 0:1], scalar=mv[:, 0:1], in1=mv[:, 1:2],
                                            op0=ALU.mult, op1=ALU.add))
                dve.wait_ge(ps_sem, b + 1)
                st(dve.tensor_copy(gstat[:], small_ps[0:C, 500:502]))
                st(dve.tensor_scalar(gpar[:, 3:4], gstat[:, 0:1], gstat[:, 0:1], None, ALU.mult))
                st(dve.scalar_tensor_tensor(out=gpar[:, col:col + 1], in0=gstat[:, 1:2], scalar=1e-5, in1=gpar[:, 3:4],
                                            op0=ALU.add, op1=ALU.subtract))
                dve.wait_ge(pow_sem, b + 1)
                st(dve.tensor_copy(par[:, 0:1], gpar[:, col:col + 1]))
                st(dve.scalar_tensor_tensor(out=par[:, 1:2], in0=gstat[:, 0:1], scalar=-1.0, in1=par[:, 0:1],
                                            op0=ALU.mult, op1=ALU.mult))

            def edge_rows(b, q):
                at = XR - PAD if q == 0 else 0
                dve.memset(xin[:, q % 2, at:at + PAD, :], 0.0).then_inc(edge_zero, 1)
                dve.wait_ge(edge_zero, b * EDGES + (1 if q == 0 else 2))

            def taps(b, u, n0=0, n1=TAPS // 2, hooks=()):
                q, ch, dirs = unit(u)
                if first_image(b):
                    dirs = [d for d in dirs if d < DIRS - 1]
                for n in range(n0, min(n1, len(dirs) * (KT - 1))):
                    k, d = n // len(dirs) + 1, dirs[n % len(dirs)]
                    dy, dx = tap_shift(d, k)
                    src = xin[:, q % 2, PAD + dy:PAD + dy + CR, PAD + dx:PAD + dx + W]
                    dst = feat[:, d].rearrange("p (r c) -> p r c", c=W)
                    if k == 1:
                        dve.wait_ge(tap_first, firsts_before(b, q) + d + 1)
                    else:
                        dve.wait_ge(tap_done, unit_taps(b, u, k - 1, d % 2))
                    dve.scalar_tensor_tensor(out=dst, in0=src, scalar=taps_w[d](k), in1=dst,
                                             op0=ALU.mult, op1=ALU.add).then_inc(tap_done, 1)
                    for at, hook in hooks:
                        if at == n + 1:
                            hook()

            def maxes(i, n0, n1):
                for n in range(n0, n1):
                    dve.wait_ge(stage_full, i * USES + n + 1)
                    dve.tensor_reduce(mx[:, n % 2, n // 2:n // 2 + 1], stage_ps[0:C, n % SLOTS, :], AX.X, ALU.max)\
                        .then_inc(max_part, 1)

            def e_split(i, t0, t1):
                for t in range(t0, t1):
                    dve.wait_ge(stage_evac, i * (USES - U_MAX) + AT_E - U_MAX + t + 1)
                    dve.tensor_copy(rows(e_hi, t * TR, TR), etile[:, t % ETILES].rearrange("p (r c) -> p r c", c=W))\
                        .then_inc(e_hi_ready, 1)
                    if t >= 1:
                        e_low(i, t - 1)

            def e_low(i, t):
                dve.wait_ge(e_hi_ready, i * U_E + t + 1)
                dve.tensor_tensor(rows(e_lo, t * TR, TR), etile[:, t % ETILES].rearrange("p (r c) -> p r c", c=W),
                                  rows(e_hi, t * TR, TR).bitcast(F32), ALU.subtract).then_inc(e_ready, 1)

            def attention_weights(i, chain):
                st = chain
                dve.wait_ge(gram_done, i + 1)
                st(dve.tensor_tensor(ctxm[:], ctx_ps[0:C, 0:C], mask, ALU.mult))
                st(dve.tensor_copy(gram0[:], gram_ps[0:C, 0:2 * C]))
                st(dve.scalar_tensor_tensor(out=gram[:], in0=gram_ps[0:C, 2 * C:4 * C], scalar=2.0, in1=gram0[:],
                                            op0=ALU.mult, op1=ALU.add))
                e_split(i, 0, 5)
                dve.wait_ge(l1_ps, i * 5 + 2)
                st(dve.tensor_tensor_reduce(junk[:], small_ps[0:C, 0:C], wq2, 1.0 / N, 0.0, ALU.mult, ALU.add,
                                            l1v[:, 0:1]))
                st(dve.reciprocal(l1v[:, 2:3], small_ps[0:C, 2 * C:2 * C + 1]))
                st(dve.tensor_scalar(s_t[:], small_ps[0:C, C:2 * C], l1v[:, 2:3], None, ALU.mult))
                st(dve.tensor_copy(m_b[:], ctx_ps[0:C, 128:128 + C]))
                dve.wait_ge(l1_pow, i + 1)
                st(dve.tensor_scalar(l1v[:, 3:4], l1v[:, 1:2], 1e-12, None, ALU.max))
                st(dve.reciprocal(l1v[:, 4:5], l1v[:, 3:4]))
                st(dve.tensor_scalar(l1v[:, 7:8], l1v[:, 4:5], temp[:, 0:1], 1.0 / N, ALU.mult, ALU.mult))
                e_split(i, 5, 7)
                dve.wait_ge(l1_ps, i * 5 + 3)
                st(dve.scalar_tensor_tensor(out=gram0[:, 0:C], in0=small_ps[0:C, 0:C], scalar=l1v[:, 7:8], in1=negmask,
                                            op0=ALU.mult, op1=ALU.add))
                st(dve.tensor_reduce(l1v[:, 5:6], gram0[:, 0:C], AX.X, ALU.max, negate=True))
                e_split(i, 7, 11)
                dve.wait_ge(l1_exp, i + 1)
                st(dve.reciprocal(l1v[:, 8:9], l1v[:, 6:7]))
                st(dve.tensor_scalar(att_f[:], junk[:], l1v[:, 8:9], None, ALU.mult))
                e_split(i, 11, 18)
                dve.wait_ge(l1_ps, i * 5 + 4)
                st(dve.tensor_tensor(bk[:], small_ps[0:C, None, 0:C].broadcast_to([C, 9, C]),
                                     wk3[:, :, None].broadcast_to([C, 9, C]), ALU.mult))
                e_split(i, 18, U_E - 1)
                dve.wait_ge(stage_evac, (i + 1) * (USES - U_MAX))
                st(dve.tensor_reduce(l1v[:, 9:10], zq[:], AX.X, ALU.add))
                st(dve.reciprocal(l1v[:, 10:11], l1v[:, 9:10]))
                st(dve.tensor_tensor(l1v[:, 11:12], l1v[:, 10:11], l1v[:, 2:3], ALU.mult))
                dve.wait_ge(l1_ps, i * 5 + 5)
                st(dve.tensor_scalar(a32[:].rearrange("p t c -> p (t c)").rearrange("p (s n) -> p s n", s=2),
                                     a_ps[0:C, :, 0:9 * C // 2], l1v[:, 11:12], None, ALU.mult))
                e_split(i, U_E - 1, U_E)
                dve.wait_ge(a_hi_ready, i + 1)
                st(dve.tensor_tensor(a_lo[:], a32[:], a_hi[:].bitcast(F32), ALU.subtract))
                e_low(i, U_E - 1)

            def x1_sum(b, j):
                s, n = j % RES, res_loads(b, j)
                dve.wait_ge(conv_ready, b * NG + j + 1)
                dve.wait_ge(*n)
                dst = x1[0:C, j * GR * W:(j + 1) * GR * W].rearrange("p (h n) -> p h n", h=2)
                dve.tensor_tensor(dst, conv_ps[0:C, j % 2, :, 0:TR * W], res[:, s].rearrange("p (h n) -> p h n", h=2),
                                  ALU.add).then_inc(x1_done, 1)
                dve.wait_ge(x1_done, b * NG + j + 1)
                for k in range(2):
                    dve.bn_stats(x1stats[:, 2 * j + k, :], dst[:, k, :]).then_inc(x1_stat, 1)

            def attention(b):
                st = small_chain(dve, l0_small, L0_SMALL, b)
                dve.wait_ge(squared, (b + 1) * DIRS * NCH)
                st(dve.tensor_reduce(l0v[:, 8:12], sq[:], AX.X, ALU.add))
                st(dve.tensor_scalar(l0v[:, 0:4], l0v[:, 8:12], 1.0 / N, None, ALU.mult))
                dve.wait_ge(l0_ps, 2 * b + 1)
                st(dve.tensor_copy(hid[:, 0:1], small_ps[0:MID, 504:505]))
                st(dve.scalar_tensor_tensor(out=hid[:, 1:2], in0=hid[:, 0:1], scalar=0.2, in1=hid[:, 0:1],
                                            op0=ALU.mult, op1=ALU.max))
                dve.wait_ge(l0_ps, 2 * b + 2)
                st(dve.tensor_copy(l0v[:, 4:8], small_ps[0:C, 506:510]))
                st(dve.tensor_reduce(l0v[:, 16:17], l0v[:, 4:8], AX.X, ALU.max, negate=True))
                dve.wait_ge(l0_exp, b + 1)
                st(dve.reciprocal(l0v[:, 18:19], l0v[:, 17:18]))
                st(dve.tensor_scalar(l0v[:, 8:12], l0v[:, 12:16], l0v[:, 18:19], None, ALU.mult))

            def products(b, ch, k0, k1, second):
                flat = acc[:].rearrange("p r c -> p (r c)")
                part = feat[:, summed(ch, 0)]
                for k in range(k0, k1):
                    d = summed(ch, k)
                    if ch >= 1:
                        dve.wait_ge(*combo_loaded(b, ch, d))
                    if k == 0:
                        ins = dve.tensor_scalar(part, part, l0v[:, 8 + d:9 + d], None, ALU.mult)
                    else:
                        dve.wait_ge(combo, (b * NCH + ch) * DIRS + k)
                        if k == DIRS - 1:
                            if ch >= 1:
                                dve.wait_ge(fg_ready, b * NCH + ch)
                            if second:
                                dve.wait_ge(fin_ready, (b - 1) * NG + min(NG, 2 * ch + 3))
                            elif ch == 0:
                                dve.wait_ge(pads_zero, PADS)
                        ins = dve.scalar_tensor_tensor(out=flat if k == DIRS - 1 else part, in0=feat[:, d],
                                                       scalar=l0v[:, 8 + d:9 + d], in1=part, op0=ALU.mult, op1=ALU.add)
                    ins.then_inc(combo, 1)

            def fg_low(b, ch):
                dve.wait_ge(fg_hi, b * NCH + ch + 1)
                dve.tensor_tensor(rows(e_lo, ch * CR, CR), acc[:], rows(e_hi, ch * CR, CR).bitcast(F32),
                                  ALU.subtract).then_inc(fg_ready, 1)

            def start(b, between=lambda: None):
                for n in range(STATS):
                    x_stats(b, n, n + 1)
                    if n % (2 * XSTAT) == 2 * XSTAT - 1 and n + 1 < STATS:
                        between()
                if first_image(b):
                    set_up()
                group_norm(b, xstats, gnx_small, gnx_ps, gnx_pow, 0, xpar, x_stat, (b + 1) * STATS)
                between()
                edge_rows(b, 0)
                taps(b, 0, hooks=[(2, between), (6, between), (10, between)])
                taps(b, 1, 0, EARLY_TAPS, hooks=[(2, between), (6, between)])

            def step(b, first, second, more):
                i = b - 1
                if second:
                    chain = small_chain(dve, l1_small, L1_SMALL, i)
                    for n in range(MAX_TAPS + 1):
                        maxes(i, n * U_MAX // (MAX_TAPS + 1), (n + 1) * U_MAX // (MAX_TAPS + 1))
                        if first and n < MAX_TAPS:
                            taps(b, 1, EARLY_TAPS + n, EARLY_TAPS + n + 1)
                    dve.wait_ge(max_part, (i + 1) * U_MAX)
                    chain(dve.tensor_reduce(nmax[:], mx[:], AX.X, ALU.max, negate=True))
                if first:
                    for u in range(2, LEAD):
                        taps(b, u)
                    dve.wait_ge(tap_done, unit_taps(b, LEAD - 1, KT - 1, 0 if first_image(b) else 1))
                    if first_image(b):
                        dve.wait_ge(last_dir_sums, LEAD)
                    edge_rows(b, NCH - 1)
                    taps(b, LEAD, 0, LEAD_TAPS)
                if second:
                    attention_weights(i, chain)
                if first:
                    taps(b, LEAD, LEAD_TAPS)
                    for u in range(LEAD + 1, UNITS):
                        taps(b, u)
                    attention(b)
                    done = [0]

                    def sums():
                        if done[0] < NG:
                            x1_sum(b, done[0])
                            done[0] += 1
                    products(b, 0, 0, 1, second)
                    for ch in range(NCH):
                        products(b, ch, 1, DIRS, second)
                        if ch + 1 < NCH:
                            products(b, ch + 1, 0, 1, second)
                        fg_low(b, ch)
                        for _ in range(SUMS_AFTER[ch]):
                            sums()
                    if more:
                        start(b + 1, sums)
                    while done[0] < NG:
                        sums()
                    group_norm(b, x1stats, gnx1_small, gnx1_ps, gnx1_pow, 2, x1par, x1_stat, (b + 1) * 2 * NG)
            steps(dve, start, step)

        @block.tensor
        def _(pe):
            pe.wait_ge(w_loaded, 24 * 16)
            pe.matmul(small_ps[0:C, 0:C], m_b[:], s_t[:], start=True, stop=True).then_inc(wc_ready, 1)
            pe.wait_ge(wc_copied, 1)
            pe.wait_ge(consts_set, 5)

            def stage(i, u):
                v = u - SLOTS
                if v < 0:
                    pass
                elif v < U_MAX:
                    pe.wait_ge(max_part, i * U_MAX + v + 1)
                else:
                    pe.wait_ge(stage_evac, i * (USES - U_MAX) + v - U_MAX + 1)
                return stage_ps[:, u % SLOTS]

            def evacuated(i, u):
                pe.wait_ge(stage_evac, i * (USES - U_MAX) + u - U_MAX + 1)

            def group_sums(b, chain, done):
                pe.wait_ge(chain, b * GN_SMALL + 2)
                pe.matmul(small_ps[0:C, 500:502], group, mv[:], start=True, stop=True).then_inc(done, 1)

            def conv(i, whi, wlo, done, ready, between={}, low_ready=lambda: None):
                for j in range(NG):
                    ready(j)
                    for h in range(2):
                        if (j, h) in between:
                            between[j, h]()
                        r0 = j * GR + h * TR

                        def tap(t):
                            dy, dx = t // 3 - 1, t % 3 - 1
                            a0, a1 = max(r0, -dy), min(r0 + TR, H - dy)
                            return conv_ps[0:C, j % 2, h, (a0 - r0) * W:(a1 - r0) * W], a0 + dy, a1 - a0, dx
                        for t in CENTRE_FIRST:
                            dst, a0, n, dx = tap(t)
                            pe.matmul(dst, whi[:, t, :], rows(e_hi, a0, n, dx), start=(t == CENTRE_FIRST[0]), stop=False)
                            pe.matmul(dst, whi[:, t, :], rows(e_lo, a0, n, dx), start=False, stop=False)
                        if (j, h) == (0, 0):
                            low_ready()
                        for t in CENTRE_LAST:
                            dst, a0, n, dx = tap(t)
                            last = pe.matmul(dst, wlo[:, t, :], rows(e_hi, a0, n, dx), start=False, stop=(t == CENTRE_LAST[-1]))
                    last.then_inc(done, 1)

            def maxes(i):
                for n in range(U_MAX):
                    t = n // 2
                    pe.wait_ge(xn_ready, i * XN + t + 1)
                    ps = stage(i, n)
                    w = wkv[0:C, 0:C] if n % 2 == 0 else wq
                    pe.matmul(ps[0:C, :], w, x1[0:C, t * BANK:(t + 1) * BANK], start=True, stop=True)\
                        .then_inc(stage_full, 1)

            def dft(i, at):
                for n, (kind, g) in enumerate(DFT_ORDER):
                    ps = stage(i, at + n)
                    if kind == 1:
                        if g == 0:
                            evacuated(i, at - 1)
                        for c in range(4):
                            last = pe.matmul(ps[0:H, c * W:(c + 1) * W], z[:, :, 4 * g + c], w_dft, start=(c == 0), stop=(c == 3),
                                             skip_group_check=True)
                    else:
                        first_of = [k for k, v in enumerate(DFT_ORDER) if v == (1, 2 * g + 1)][0]
                        evacuated(i, at + first_of)
                        d = ps[0:H, 0:8 * NV].rearrange("p (c v) -> p c v", v=NV)
                        pe.matmul(d, dcos, s1[:, g % 2, :, 0:NV], start=True, stop=False)
                        last = pe.matmul(d[:, :, 1:NV - 1], dnsin, s1[:, g % 2, :, NV:W], start=False, stop=True)
                    last.then_inc(stage_full, 1)

            def ctx_rows(i, g):
                evacuated(i, AT_KV + g)
                for r in range(2):
                    last = pe.matmul(ctx_ps[0:C, 0:C], vrow[:, g % VROWS, r, :], z[:, 2 * g + r, :],
                                     start=(g == 0 and r == 0), stop=(g == U_KV - 1 and r == 1))
                return last

            def q_tiles(i, t0, t1):
                for t in range(t0, t1):
                    ps = stage(i, AT_E + t)
                    pe.matmul(ps[0:C, 0:TR * W], wq, x1[0:C, t * TR * W:(t + 1) * TR * W], start=True, stop=True)\
                        .then_inc(stage_full, 1)

            def attention_block(i, between):
                maxes(i)
                for g in range(U_ROWS):
                    ps = stage(i, AT_ROWS + g)
                    for r in range(TR):
                        h = g * TR + r
                        last = pe.matmul(ps[0:W, r * C:(r + 1) * C], x1[0:C, h * W:(h + 1) * W], wq1,
                                         start=(r == 0), stop=(r == TR - 1), skip_group_check=True)
                    last.then_inc(stage_full, 1)
                pe.wait_ge(l1_small, i * L1_SMALL + 1)
                pe.matmul(small_ps[0:1, 0:C], nmax[:, 0:1], ident, start=True, stop=True).then_inc(l1_ps, 1)
                dft(i, AT_DFT1)
                pe.wait_ge(maxrow_ready, i + 1)
                wait(pe, x1_done, (i + 1) * NG)
                for g in range(U_KV + BEHIND):
                    if g < U_KV:
                        ps = stage(i, AT_KV + g)
                        for r in range(2):
                            h = 2 * g + r
                            last = pe.matmul(ps[0:W, r * 2 * C:(r + 1) * 2 * C], x1[:, h * W:(h + 1) * W], wkv[:],
                                             start=(r == 0), stop=(r == 1), skip_group_check=True)
                        last.then_inc(stage_full, 1)
                    if g >= BEHIND:
                        ctx_rows(i, g - BEHIND)
                dft(i, AT_DFT2)
                evacuated(i, AT_DFT2 + U_DFT - 1)
                for v in (0, NV - 1):
                    pe.matmul(gram_ps[0:C, 0:2 * C], t_sp[:, v, 0:C], t_sp[:, v, :], start=(v == 0), stop=(v != 0))
                for v in range(1, NV - 1):
                    pe.matmul(gram_ps[0:C, 2 * C:4 * C], t_sp[:, v, 0:C], t_sp[:, v, :], start=(v == 1), stop=(v == NV - 2))
                pe.matmul(small_ps[0:C, 2 * C:2 * C + 1], t_sp[0:1, 0, C:2 * C], one[0:1, 0:1], start=True, stop=True)\
                    .then_inc(gram_done, 1)
                q_tiles(i, 0, 7)
                pe.wait_ge(l1_small, i * L1_SMALL + 4)
                pe.matmul(small_ps[0:C, 0:C], wq2t, gram[:, 0:C], start=True, stop=True)
                pe.matmul(small_ps[0:C, C:2 * C], gram[:, C:2 * C], wq2t, start=True, stop=True)
                pe.matmul(ctx_ps[0:C, 128:128 + C], wc[:], ctxm[:], start=True, stop=True).then_inc(l1_ps, 1)
                q_tiles(i, 7, 10)
                pe.wait_ge(l1_small, i * L1_SMALL + 7)
                pe.matmul(small_ps[0:C, 0:C], s_t[:], ident, start=True, stop=True).then_inc(l1_ps, 1)
                q_tiles(i, 10, 17)
                pe.wait_ge(l1_small, i * L1_SMALL + 15)
                pe.matmul(small_ps[0:C, 0:C], att_f[:], wpft, start=True, stop=True).then_inc(l1_ps, 1)
                q_tiles(i, 17, U_E)
                pe.wait_ge(l1_small, i * L1_SMALL + 16)
                flat = bk[:].rearrange("p t c -> p (t c)")
                half = 9 * C // 2
                pe.matmul(a_ps[0:C, 0, 0:half], m_b[:], flat[:, 0:half], start=True, stop=True)
                pe.matmul(a_ps[0:C, 1, 0:half], m_b[:], flat[:, half:2 * half], start=True, stop=True).then_inc(l1_ps, 1)

                def ready(j):
                    pe.wait_ge(e_ready, i * U_E + min(U_E, (j + 1) * GR // TR + 1))
                    if j == 0:
                        pe.wait_ge(a_hi_ready, i + 1)
                    elif j >= 2:
                        pe.wait_ge(fin_copied, i * NG + j - 1)
                conv(i, a_hi, a_lo, fin_ready, ready, between, lambda: pe.wait_ge(l1_small, i * L1_SMALL + 21))

            def start(b):
                group_sums(b, gnx_small, gnx_ps)

            def last_direction():
                pe.wait_ge(diag_ready, KT)
                for q in range(NCH):
                    pe.wait_ge(xin_ready, q + 1)
                    if q == 0 or q == NCH - 1:
                        pe.wait_ge(edge_zero, 1 if q == 0 else EDGES)
                    for half in range(2):
                        if q >= 1:
                            pe.wait_ge(last_dir_made, 2 * (q - 1) + half + 1)
                        for h in range(2):
                            for k in range(KT):
                                dy, dx = tap_shift(DIRS - 1, k)
                                r0 = PAD + dy + (2 * half + h) * TR
                                last = pe.matmul(conv_ps[0:C, half, h, 0:TR * W], bk[:, k, :],
                                                 xin[:, q % 2, r0:r0 + TR, PAD + dx:PAD + dx + W],
                                                 start=(k == 0), stop=(k == KT - 1))
                        last.then_inc(last_dir_sums, 1)

            def step(b, first, second, more):
                if first_image(b):
                    last_direction()
                def hidden():
                    pe.wait_ge(l0_small, b * L0_SMALL + 2)
                    for d in range(DIRS):
                        last = pe.matmul(small_ps[0:MID, 504:505], att1[:, d, :], l0v[:, d:d + 1], start=(d == 0),
                                         stop=(d == DIRS - 1))
                    last.then_inc(l0_ps, 1)

                def logits():
                    pe.wait_ge(l0_small, b * L0_SMALL + 4)
                    for d in range(DIRS):
                        last = pe.matmul(small_ps[0:C, 506 + d:507 + d], att2[:, d * C:(d + 1) * C], hid[:, 1:2],
                                         start=True, stop=True)
                    last.then_inc(l0_ps, 1)

                if second:
                    attention_block(b - 1, {(HID_AT, 1): hidden, (HID_AT + 1, 0): logits} if first else {})
                elif first:
                    hidden()
                    logits()
                if first:
                    if not second:
                        pe.wait_ge(wp_ready, 1)

                    def ready(j):
                        pe.wait_ge(fg_ready, b * NCH + min(NCH - 1, (j + 1) * GR // CR) + 1)
                        if j < 2:
                            if second:
                                pe.wait_ge(fin_copied, (b - 1) * NG + NG - 1 + j)
                        else:
                            pe.wait_ge(x1_done, b * NG + j - 1)
                    conv(b, wp_hi, wp_lo, conv_ready, ready, {(GN_AT + 1, 0): lambda: start(b + 1)} if more else {})
                    group_sums(b, gnx1_small, gnx1_ps)
            steps(pe, start, step)


NAMES = ["x", "ident", "group", "mask", "negmask", "w_dft", "dcos", "dnsin", "wq", "wq1", "wq2", "wq2t", "wpft",
         "wkv", "wh", "wv", "w45", "w135", "wk3", "temp", "att1", "att2", "wp", "w_mid", "wkvv"]


def kernel(x, L0_conv_w_h, L0_conv_w_v, L0_conv_w_d45, L0_conv_w_d135, L0_conv_w_att1, L0_conv_w_att2,
           L0_conv_w_proj, L1_conv_temperature, L1_conv_w_qkv, L1_conv_w_proj, L1_conv_w_kv, L1_conv_w_q1,
           L1_conv_w_q2, L1_conv_w_kvconv, L1_conv_w_projf):
    import numpy as np
    import concourse.bacc as bacc
    from concourse.bass_utils import run_bass_kernel_spmd

    f = np.float32
    n = np.arange(W)
    angle = 2 * np.pi * np.outer(n, n) / W
    cos, sin = np.cos(angle), np.sin(angle)
    head = n // HD
    same = head[:, None] == head[None, :]
    grp = n // 3
    qkv = np.asarray(L1_conv_w_qkv)
    t = {
        "x": np.asarray(x).reshape(B, C, N),
        "ident": np.eye(C).astype(f),
        "group": ((grp[:, None] == grp[None, :]) / 3.0).astype(f),
        "mask": same.astype(f),
        "negmask": np.where(same, 0.0, -1e30).astype(f),
        "w_dft": np.concatenate([cos[:, :NV], sin[:, 1:NV - 1]], 1).astype(f),
        "dcos": cos.astype(f),
        "dnsin": (-sin).astype(f),
        "wq": qkv[0:C].T, "wkv": qkv[C:3 * C].T,
        "wq1": np.asarray(L1_conv_w_q1).T, "wq2": np.asarray(L1_conv_w_q2), "wq2t": np.asarray(L1_conv_w_q2).T,
        "wpft": np.asarray(L1_conv_w_projf).T,
        "wh": np.asarray(L0_conv_w_h).reshape(C, KT), "wv": np.asarray(L0_conv_w_v).reshape(C, KT),
        "w45": np.asarray(L0_conv_w_d45).reshape(C, KT * KT), "w135": np.asarray(L0_conv_w_d135).reshape(C, KT * KT),
        "wk3": np.asarray(L1_conv_w_kvconv)[C:].reshape(C, 9),
        "temp": np.repeat(np.asarray(L1_conv_temperature).reshape(HEADS, 1), HD, 0),
        "att1": np.asarray(L0_conv_w_att1).reshape(MID, DIRS, C).transpose(2, 1, 0),
        "att2": np.asarray(L0_conv_w_att2).T,
        "wp": np.asarray(L0_conv_w_proj).transpose(1, 2, 3, 0).reshape(C, 9, C),
        "w_mid": np.asarray(L1_conv_w_proj),
        "wkvv": np.asarray(L1_conv_w_kv)[C:].T,
    }
    nc = bacc.Bacc("TRN2", target_bir_lowering=False, num_devices=1)
    arrays, aps = {}, {}
    for name in NAMES:
        arrays["in_" + name] = np.ascontiguousarray(t[name])
        aps[name] = nc.dram_tensor("in_" + name, arrays["in_" + name].shape, F32, kind="ExternalInput").ap()
    out = nc.dram_tensor("out", (B, C, N), F32, kind="ExternalOutput").ap()
    build(nc, aps, out)
    r = run_bass_kernel_spmd(nc, [arrays], core_ids=[0])
    return r.results[0]["out"].reshape(B, C, H, W)
```
